# Optimizing a Trainium2 kernel written in Bass

```python
import numpy as np
import jax
import jax.numpy as jnp

def _softmax(x, axis=-1):
    return jax.nn.softmax(x, axis=axis)

def _gelu(x):
    return jax.nn.gelu(x, approximate=True)

def _silu(x):
    return jax.nn.silu(x)

def _sigmoid(x):
    return jax.nn.sigmoid(x)

def _layernorm(x, axis=-1, eps=1e-05):
    m = jnp.mean(x, axis=axis, keepdims=True)
    v = jnp.var(x, axis=axis, keepdims=True)
    return (x - m) / jnp.sqrt(v + eps)

def _scatter_add(tgt, idx, src, axis=0):
    return tgt.at[idx].add(src)

def _segment_sum(src, seg, n):
    return jax.ops.segment_sum(src, seg, n)
kernel_name = 'mk_adaln_d1_jaxref_r8_9aa6c8'

def setup_inputs(seed: int=0):
    np.random.seed(seed)
    _w = jnp.asarray

    def _L0_attn_setup():
        import jax, jax.numpy as jnp
        from jax import lax
        import numpy as np
        D_MODEL = 256
        D_INNER = 256
        D_STATE = 64
        NH = 32
        HEADDIM = D_INNER // NH
        D_CONV = 4
        CONV_DIM = D_INNER + 2 * NH * D_STATE
        IN_DIM = 2 * D_INNER + 2 * NH * D_STATE + NH
        B_SZ, L_SEQ = (2, 128)

        def segsum(a):
            T = a.shape[-1]
            strict = jnp.tril(jnp.ones((T, T), bool), -1)
            X = jnp.where(strict, a[..., :, None], 0.0)
            S = jnp.cumsum(X, axis=-2)
            keep = jnp.tril(jnp.ones((T, T), bool))
            return jnp.where(keep, S, -jnp.inf)
        key = jax.random.key(seed)
        ks = jax.random.split(key, 5)
        s = 0.02
        return {'u': jax.random.normal(ks[0], (B_SZ, L_SEQ, D_MODEL), jnp.float32), 'W_in': jax.random.normal(ks[1], (IN_DIM, D_MODEL), jnp.float32) * s, 'conv_w': jax.random.normal(ks[2], (CONV_DIM, 1, D_CONV), jnp.float32) * 0.2, 'conv_b': jnp.zeros((CONV_DIM,), jnp.float32), 'z_bias': jnp.zeros((D_INNER,), jnp.float32), 'D': jnp.ones((NH,), jnp.float32), 'W_out': jax.random.normal(ks[3], (D_MODEL, D_INNER), jnp.float32) * s}
    _L0_attn_in = _L0_attn_setup()

    def _L0_ffn_setup():
        import jax, jax.numpy as jnp
        import numpy as np
        B, S, D, H = (4, 256, 256, 1024)

        def fwht(x):
            orig_shape = x.shape
            n = orig_shape[-1]
            x = x.reshape(-1, n)
            h = 1
            while h < n:
                xb = x.reshape(-1, n // (2 * h), 2, h)
                a = xb[:, :, 0, :]
                b = xb[:, :, 1, :]
                x = jnp.stack([a + b, a - b], axis=2).reshape(-1, n)
                h *= 2
            scale = jnp.asarray(1.0 / np.sqrt(n), dtype=x.dtype)
            return (x * scale).reshape(orig_shape)
        key = jax.random.key(seed)
        kx, k1, k2, k3 = jax.random.split(key, 4)
        x = jax.random.normal(kx, (B, S, D), dtype=jnp.float32)
        W1 = jax.random.normal(k1, (H, D), dtype=jnp.float32) * (1.0 / np.sqrt(D))
        W2 = jax.random.normal(k2, (D, H), dtype=jnp.float32) * (1.0 / np.sqrt(H))
        W3 = jax.random.normal(k3, (H, D), dtype=jnp.float32) * (1.0 / np.sqrt(D))
        return {'x': x, 'W1': W1, 'W2': W2, 'W3': W3}
    _L0_ffn_in = _L0_ffn_setup()
    _L0_c = _w((lambda *s: np.random.randn(*s).astype(np.float32) * 0.05)(4, 256))
    _L0_wmod = _w((lambda *s: np.random.randn(*s).astype(np.float32) * 0.05)(256, 6 * 256) * 256 ** (-0.5))
    _d = {'L0_attn_u': _L0_attn_in['u'], 'L0_attn_W_in': _L0_attn_in['W_in'], 'L0_attn_conv_w': _L0_attn_in['conv_w'], 'L0_attn_conv_b': _L0_attn_in['conv_b'], 'L0_attn_z_bias': _L0_attn_in['z_bias'], 'L0_attn_D': _L0_attn_in['D'], 'L0_attn_W_out': _L0_attn_in['W_out'], 'L0_ffn_W1': _L0_ffn_in['W1'], 'L0_ffn_W2': _L0_ffn_in['W2'], 'L0_ffn_W3': _L0_ffn_in['W3'], 'L0_c': _L0_c, 'L0_wmod': _L0_wmod}
    _x0 = _d['L0_attn_u']
    _d['L0_attn_u'] = jax.random.normal(jax.random.fold_in(jax.random.key(seed), 1), (4, 512, 256), dtype=_x0.dtype)
    del _x0
    return _d

def reference(L0_attn_u, L0_attn_W_in, L0_attn_conv_w, L0_attn_conv_b, L0_attn_z_bias, L0_attn_D, L0_attn_W_out, L0_ffn_W1, L0_ffn_W2, L0_ffn_W3, L0_c, L0_wmod):

    def _L0_attn_ref(u, W_in, conv_w, conv_b, z_bias, D, W_out):
        import jax, jax.numpy as jnp
        from jax import lax
        import numpy as np
        D_MODEL = 256
        D_INNER = 256
        D_STATE = 64
        NH = 32
        HEADDIM = D_INNER // NH
        D_CONV = 4
        CONV_DIM = D_INNER + 2 * NH * D_STATE
        IN_DIM = 2 * D_INNER + 2 * NH * D_STATE + NH
        B_SZ, L_SEQ = (2, 128)

        def segsum(a):
            T = a.shape[-1]
            strict = jnp.tril(jnp.ones((T, T), bool), -1)
            X = jnp.where(strict, a[..., :, None], 0.0)
            S = jnp.cumsum(X, axis=-2)
            keep = jnp.tril(jnp.ones((T, T), bool))
            return jnp.where(keep, S, -jnp.inf)
        b, l, _ = u.shape
        proj = u @ W_in.T
        xBC, z, A_log = jnp.split(proj, [CONV_DIM, CONV_DIM + D_INNER], axis=-1)
        xc = lax.conv_general_dilated(xBC.transpose(0, 2, 1), conv_w, (1,), [(D_CONV - 1, 0)], feature_group_count=CONV_DIM)
        xBC = (xc + conv_b[None, :, None]).transpose(0, 2, 1)
        x, Bm, Cm = jnp.split(xBC, [D_INNER, D_INNER + NH * D_STATE], axis=-1)
        x = x.reshape(b, l, NH, HEADDIM)
        Bm = Bm.reshape(b, l, NH, D_STATE)
        Cm = Cm.reshape(b, l, NH, D_STATE)
        a = -jax.nn.softplus(A_log).transpose(0, 2, 1)
        Lm = jnp.exp(segsum(a))
        M = jnp.einsum('blhn,bshn,bhls->bhls', Cm, Bm, Lm)
        y = jnp.einsum('bhls,bshp->blhp', M, x)
        y = y + D[None, None, :, None] * x
        y = y.reshape(b, l, D_INNER)
        out = y * jax.nn.silu(z + z_bias) @ W_out.T
        return out

    def _L0_ffn_ref(x, W1, W2, W3):
        import jax, jax.numpy as jnp
        import numpy as np
        B, S, D, H = (4, 256, 256, 1024)

        def fwht(x):
            orig_shape = x.shape
            n = orig_shape[-1]
            x = x.reshape(-1, n)
            h = 1
            while h < n:
                xb = x.reshape(-1, n // (2 * h), 2, h)
                a = xb[:, :, 0, :]
                b = xb[:, :, 1, :]
                x = jnp.stack([a + b, a - b], axis=2).reshape(-1, n)
                h *= 2
            scale = jnp.asarray(1.0 / np.sqrt(n), dtype=x.dtype)
            return (x * scale).reshape(orig_shape)
        up_gate = jnp.einsum('bsd,hd->bsh', x, W1)
        up_lin = jnp.einsum('bsd,hd->bsh', x, W3)
        hidden = jax.nn.silu(up_gate) * up_lin
        hidden = fwht(hidden)
        out = jnp.einsum('bsh,dh->bsd', hidden, W2)
        return out
    x = L0_attn_u
    mod = (_silu(L0_c) @ L0_wmod).reshape(L0_c.shape[0], 6, 1, -1)
    sa, ca, ga, sb, cb, gb = (mod[:, 0], mod[:, 1], mod[:, 2], mod[:, 3], mod[:, 4], mod[:, 5])
    ga = (2 * (ga >= 0) - 1) * jnp.maximum(jnp.abs(ga), 0.25)
    gb = (2 * (gb >= 0) - 1) * jnp.maximum(jnp.abs(gb), 0.25)
    h = _layernorm(x, axis=-1) * (1 + ca) + sa
    x = x + ga * _L0_attn_ref(h, L0_attn_W_in, L0_attn_conv_w, L0_attn_conv_b, L0_attn_z_bias, L0_attn_D, L0_attn_W_out)
    h = _layernorm(x, axis=-1) * (1 + cb) + sb
    x = x + gb * _L0_ffn_ref(h, L0_ffn_W1, L0_ffn_W2, L0_ffn_W3)
    return x

_drawn_inputs = setup_inputs


def setup_inputs(seed=0):
    import zlib

    import numpy as np

    out = dict(_drawn_inputs(seed))
    spreads = {'L0_attn_conv_b': (0.0, 0.1), 'L0_attn_z_bias': (0.0, 0.1), 'L0_attn_D': (1.0, 0.2)}
    factors = {}
    for name, (base, spread) in spreads.items():
        noise = np.random.default_rng([zlib.crc32(name.encode()), seed]).standard_normal(out[name].shape)
        drawn = base * np.exp(spread * noise) if base else spread * noise
        out[name] = jnp.asarray(drawn.astype(out[name].dtype))
    for name, factor in factors.items():
        out[name] = (out[name] * factor).astype(out[name].dtype)
    return out
```

```python
from contextlib import ExitStack

import concourse.bass as bass
from concourse import mybir

F32 = mybir.dt.float32
F32R = mybir.dt.float32r
BF16 = mybir.dt.bfloat16
ALU = mybir.AluOpType
ACT = mybir.ActivationFunctionType

P = 128
B, L, D = 4, 512, 256
NH, HD, NS = 32, 8, 64
HID = 1024
TAPS = 4
KT = D // P
CH = L // P
TT = B * CH
JH = 4
NG = NH // JH
GT = 4
GC = JH * HD
NM = HID // P
BANK = 512
EPS = 1e-5
V0 = [0, 3, 5]
NV = 6


def adaln_ssm_ffn_kernel(nc, u, w_bc, w_x, w_a, w_z, conv, d_rows, z_bias, w_out, w13, w2, c_t, wmod,
                         consts, head_hot, out):
    with ExitStack() as ctx:
        def sb(name, shape, dt, where=ctx):
            return where.enter_context(nc.sbuf_tensor(name, shape, dt))

        def sem(name):
            return ctx.enter_context(nc.semaphore(name))

        ps = ctx.enter_context(nc.psum_tensor("ps", [P, 8, BANK], F32))

        ht_hi = sb("ht_hi", [P, KT, B * L], F32R)
        ht_lo = sb("ht_lo", [P, KT, B * L], F32R)
        x_tok = sb("x_tok", [P, TT, D], F32)
        cst = sb("cst", [P, 5, P], F32)
        ident, triu, strict, ones, hadamard = (cst[:, i, :] for i in range(5))
        wo_sb = sb("wo_sb", [P, KT, D], F32)
        wz_raw = sb("wz_raw", [P, 2, KT, P], F32)
        wz_hi = sb("wz_hi", [P, 2, KT, P], F32R)
        wz_lo = sb("wz_lo", [P, 2, KT, P], F32R)
        zb_sb = sb("zb_sb", [P, 2], F32)
        gates = sb("gates", [P, B, 2, D], F32)
        shift = sb("shift", [P, 2, KT, B], F32)
        scale1 = sb("scale1", [P, 2, KT, B], F32)
        stats = sb("stats", [P, CH, 6], F32)
        meanvar = sb("meanvar", [P, CH, 2], F32)
        vareps = sb("vareps", [P, CH], F32)
        rstd = sb("rstd", [P, CH], F32)
        minus_half = sb("minus_half", [P, CH], F32)
        ident_bf = sb("ident_bf", [P, P], BF16)
        stage = sb("stage", [P, 2 * NM * D], F32)

        reg_a = ExitStack()
        wmod_sb = sb("wmod_sb", [P, KT, 6 * D], F32, reg_a)
        u_sb = sb("u_sb", [P, TT, D], F32, reg_a)
        xn = sb("xn", [P, 2, CH, D], F32, reg_a)
        wx_raw = sb("wx_raw", [P, 2, KT, P], F32, reg_a)
        wx_hi = sb("wx_hi", [P, 2, KT, P], F32R, reg_a)
        wx_lo = sb("wx_lo", [P, 2, KT, P], F32R, reg_a)
        h32 = sb("h32", [P, KT, L], F32, reg_a)
        reg_a.close()
        w13_hi = sb("w13_hi", [P, NM, 2, KT, P], F32R)
        w13_lo = sb("w13_lo", [P, NM, 2, KT, P], F32R)
        w2_hi = sb("w2_hi", [P, NM, D], F32R)
        w2_lo = sb("w2_lo", [P, NM, D], F32R)

        reg_b = ExitStack()
        c_sb = sb("c_sb", [P, KT, B], F32, reg_b)
        c_exp = sb("c_exp", [P, KT, B], F32, reg_b)
        c_silu = sb("c_silu", [P, KT, B], F32, reg_b)
        p_tok = sb("p_tok", [P, TT, NH], F32, reg_b)
        e_tok = sb("e_tok", [P, TT, NH], F32, reg_b)
        dec = sb("dec", [P, NV, B, NH], F32, reg_b)
        pT = sb("pT", [3 * NH, TT * P], BF16, reg_b)
        sel = sb("sel", [3 * NH, NH, P], BF16, reg_b)
        hot_sb = sb("hot_sb", [3 * NH, NH], F32, reg_b)
        conv_sb = sb("conv_sb", [P, NG * GT + 2, TAPS + 1], F32, reg_b)
        d_sb = sb("d_sb", [P, NH], F32, reg_b)
        wg_raw = sb("wg_raw", [P, GT, KT, P], F32, reg_b)
        wg_hi = sb("wg_hi", [P, GT, KT, P], F32R, reg_b)
        wg_lo = sb("wg_lo", [P, GT, KT, P], F32R, reg_b)
        cw_act = sb("cw_act", [P, GT, 2], F32, reg_b)
        cw_dve = sb("cw_dve", [P, GT, 3], F32, reg_b)
        p_slot = sb("p_slot", [P, TT, JH], F32, reg_b)
        acc = sb("acc", [P, 2, GT, L], F32, reg_b)
        decay = sb("decay", [P, JH, L], F32, reg_b)
        reg_c = ExitStack()
        c_rows = sb("c_rows", [P, KT, B, P], F32, reg_c)
        a_abs = sb("a_abs", [P, TT * NH], F32, reg_c)
        a_exp = sb("a_exp", [P, TT * NH], F32, reg_c)
        parts = sb("parts", [P, TT, 3, NH], BF16, reg_c)
        wa_raw = sb("wa_raw", [P, KT, NH], F32, reg_c)
        wa_hi = sb("wa_hi", [P, KT, NH], F32R, reg_c)
        wa_lo = sb("wa_lo", [P, KT, NH], F32R, reg_c)
        sp_a = sb("sp_a", [P, B, CH, NH], F32, reg_c)
        reg_c.close()
        mix = sb("mix", [P, JH, L], F32, reg_b)
        b_tok = sb("b_tok", [P, 2, 3 * P], F32, reg_b)
        yt_sb = sb("yt_sb", [2 * GC, L], F32, reg_b)
        xds = sb("xds", [P, 2, NV, GC], F32, reg_b)
        st_sb = sb("st_sb", [P, 2, 3, GC], F32, reg_b)
        xs = sb("xs", [P, 2, JH * (P + HD)], F32, reg_b)
        y_off = sb("y_off", [P, 3, GC], F32, reg_b)
        reg_b.close()
        hid_hi = sb("hid_hi", [P, NM, L], F32R)
        hid_lo = sb("hid_lo", [P, NM, L], F32R)
        hid = sb("hid", [P, 2, L], F32)
        silu_sb = sb("silu_sb", [P, 2, L], F32)
        yv = sb("yv", [P, CH, D], F32)
        sz = sb("sz", [P, KT, L], F32)
        gy = sb("gy", [P, KT, L], F32)
        xn2 = sb("xn2", [P, CH, D], F32)
        h32b = sb("h32b", [P, KT, L], F32)
        h2_hi = sb("h2_hi", [P, KT, L], F32R)
        h2_lo = sb("h2_lo", [P, KT, L], F32R)
        u2 = sb("u2", [P, CH, D], F32)
        ga_out = stage[:, 0:4 * D].rearrange("p (n c d) -> p n c d", n=2, c=2)
        gb_out = stage[:, 4 * D:6 * D].rearrange("p (n c d) -> p n c d", n=2, c=1)

        names = """
        ld_c ld_wmod ld_u0 ld_u1 ld_u2 ld_u3 ld_cst ld_wx ld_wa ld_conv ld_hot sel_done ld_d ld_wg ld_wz ld_zb ld_wo
        ld_w13 ld_w2 ld_res st_out
        c_exp_done c_one c_rec c_silu_done c_rows_done mod_mm mod_ev gate_mm gate_sign gate_abs gate_ev2 gate_ev
        bnst bnag eps1 rs half_set xn_done lnT_mm h32_done hhi_done hlo_done wx_split wa_split wz_split
        xp_mm xtap xtaps xT_mm xtok_ev a_mm abs_done aexp_done aln_done sp_done ptok_mm dk_mm
        e_done dec_done p_copy part_step parts_done pT_mm pT_ev st_zero
        wraw_free w_split cwa cwd p_sl pool_waits dve_waits pe_waits proj tap0 taps bt bt_ev csb diff_done exp_done score mixed state st_copy masked
        xds_done xs_done xd_done inter intra yt_ev y_tok xs_zero yoff_done y_mid y_done
        w13_hi_done w13_split bfly w2_mm w2_hi_done w2_split
        yv_done z_mm yT_mm silu_z gated oproj res_mul x1_done bn2 ag2 eps2 rs2 xn2_done lnT2 h32b_done h2hi_done h2lo_done
        up_mm silu_done hid_done hhi2 hlo2 down_mm out_mul x2_done
        """.split()
        s = {n: sem(n) for n in names}

        block = ctx.enter_context(nc.Block())

        @block.sync
        def _(sp):
            def load(dst, src, name):
                sp.dma_start(dst, src).then_inc(s[name], 16)

            u_b = u.rearrange("(b c p) d -> b p c d", b=B, p=P)
            out_b = out.rearrange("(b c p) d -> b p c d", b=B, p=P)
            load(c_sb[:], c_t, "ld_c")
            load(u_sb[:, 0:CH, :], u_b[0], "ld_u0")
            load(cst[:], consts, "ld_cst")
            load(wmod_sb[:], wmod, "ld_wmod")
            load(wx_raw[:], w_x, "ld_wx")
            load(wa_raw[:], w_a, "ld_wa")
            load(conv_sb[:], conv, "ld_conv")
            for b in range(1, B):
                load(u_sb[:, b * CH:(b + 1) * CH, :], u_b[b], f"ld_u{b}")
            load(wg_raw[:], w_bc[0], "ld_wg")
            load(hot_sb[:], head_hot, "ld_hot")
            load(d_sb[:], d_rows, "ld_d")
            load(wz_raw[:], w_z, "ld_wz")
            load(zb_sb[:], z_bias, "ld_zb")
            load(wo_sb[:], w_out, "ld_wo")
            load(stage[:], w13, "ld_w13")
            with sp.Fori(1, NG) as g:
                sp.wait_ge(s["w_split"], g * (2 * GT))
                sp.dma_start(wg_raw[:], w_bc[bass.ds(g, 1)].rearrange("a p t k m -> p (a t) k m")).then_inc(s["ld_wg"], 16)
            sp.wait_ge(s["w13_split"], NM)
            load(stage[:, 0:NM * D], w2, "ld_w2")
            sp.wait_ge(s["y_done"], NG * B)
            for b in range(B):
                if b:
                    sp.wait_ge(s["x1_done"], 2 * b)
                load(u2[:], u_b[b], "ld_res")
            for b in range(B):
                sp.wait_ge(s["x2_done"], CH * (b + 1))
                sp.dma_start(out_b[b], x_tok[:, b * CH:(b + 1) * CH, :]).then_inc(s["st_out"], 16)
            sp.wait_ge(s["st_out"], 16 * B)

        @block.tensor
        def _(pe):
            mm = nc.tensor.matmul

            def split_mm(o, w_hi, w_lo, x_hi, x_lo, first, last):
                mm(o, w_hi, x_hi, start=first, stop=False)
                mm(o, w_hi, x_lo, start=False, stop=False)
                return mm(o, w_lo, x_hi, start=False, stop=last)

            pe.wait_ge(s["ld_wmod"], 16)
            pe.wait_ge(s["c_silu_done"], 1)
            for k, kind in enumerate((0, 1, 3, 4)):
                for m in range(KT):
                    o = ps[:, 0, (2 * k + m) * B:(2 * k + m + 1) * B]
                    for kt in range(KT):
                        i = mm(o, wmod_sb[:, kt, kind * D + m * P:kind * D + (m + 1) * P], c_silu[:, kt, :],
                               start=(kt == 0), stop=(kt == KT - 1))
            i.then_inc(s["mod_mm"], 1)
            pe.wait_ge(s["ld_cst"], 16)

            def norm_transposes(b):
                pe.wait_ge(s["xn_done"], CH * (b + 1))
                if b:
                    pe.wait_ge(s["h32_done"], KT * b)
                for c in range(CH):
                    for kt in range(KT):
                        i = nc.tensor.transpose(ps[:, 2 + kt, c * P:(c + 1) * P],
                                                xn[:, b % 2, c, kt * P:(kt + 1) * P], ident)
                i.then_inc(s["lnT_mm"], 1)

            def gate_rows(b):
                for k, kind in enumerate((2, 5)):
                    for kt in range(KT):
                        i = mm(ps[:, 4 + b, k * D:(k + 1) * D], c_rows[:, kt, b, :],
                               wmod_sb[:, kt, kind * D:(kind + 1) * D], start=(kt == 0), stop=(kt == KT - 1))
                i.then_inc(s["gate_mm"], 1)

            def x_project(b):
                pe.wait_ge(s["hlo_done"], KT * (b + 1))
                for xt in range(2):
                    n = 2 * b + xt
                    if n >= 2:
                        pe.wait_ge(s["xtaps"], 3 * (n - 1))
                    for kt in range(KT):
                        i = split_mm(ps[:, xt, :], wx_hi[:, xt, kt, :], wx_lo[:, xt, kt, :],
                                     ht_hi[:, kt, b * L:(b + 1) * L], ht_lo[:, kt, b * L:(b + 1) * L],
                                     kt == 0, kt == KT - 1)
                    i.then_inc(s["xp_mm"], 1)

            def a_project(b):
                for c in range(CH):
                    t = b * CH + c
                    for kt in range(KT):
                        i = split_mm(ps[:, 6, t * NH:(t + 1) * NH],
                                     ht_hi[:, kt, t * P:(t + 1) * P], ht_lo[:, kt, t * P:(t + 1) * P],
                                     wa_hi[:, kt, :], wa_lo[:, kt, :], kt == 0, kt == KT - 1)
                if b == B - 1:
                    i.then_inc(s["a_mm"], 1)

            def x_transposes(b):
                for xt in range(2):
                    n = 2 * b + xt
                    pe.wait_ge(s["xtaps"], 3 * (n + 1))
                    if n >= 2:
                        pe.wait_ge(s["xtok_ev"], n - 1)
                    for c in range(CH):
                        i = nc.tensor.transpose(ps[:, 4 + xt, c * P:(c + 1) * P],
                                                acc[:, n // GT, n % GT, c * P:(c + 1) * P], ident)
                    i.then_inc(s["xT_mm"], 1)

            norm_transposes(0)
            pe.wait_ge(s["c_rows_done"], KT * B)
            for b in range(B):
                gate_rows(b)
            pe.wait_ge(s["mod_ev"], 2)
            pe.wait_ge(s["wx_split"], 2)
            pe.wait_ge(s["wa_split"], 2)
            for b in range(B):
                if b + 1 < B:
                    norm_transposes(b + 1)
                x_project(b)
                if b == 0:
                    pe.wait_ge(s["gate_ev"], 1)
                a_project(b)
                if b:
                    x_transposes(b - 1)
            x_transposes(B - 1)

            pe.wait_ge(s["sp_done"], 1)
            mm(ps[:, 7, :], triu, sp_a[:].rearrange("p b c h -> p (b c h)"), start=True,
               stop=True).then_inc(s["ptok_mm"], 1)
            pe.wait_ge(s["xtok_ev"], 2 * B)
            for c in range(CH - 1):
                for t in range(CH - 1 - c):
                    v = V0[c] + t
                    o = ps[:, 4 + v // 3, (v % 3) * B * NH:(v % 3 + 1) * B * NH]
                    i = mm(o, strict, sp_a[:, :, c, :], start=True, stop=(t == 0))
                    for k in range(t):
                        i = mm(o, ones, sp_a[:, :, c + 1 + k, :], start=False, stop=(k == t - 1))
            i.then_inc(s["dk_mm"], 1)
            pe.wait_ge(s["parts_done"], 1)
            pe.wait_ge(s["xtaps"], 3 * 2 * B)
            part_ps = ps[:, 2:4, :].rearrange("p k n -> p (k n)").bitcast(BF16)
            for t in range(TT):
                i = nc.tensor.transpose(part_ps[0:3 * NH, t * P:(t + 1) * P],
                                        parts[:, t, :, :].rearrange("p k h -> p (k h)"), ident_bf[:])
            i.then_inc(s["pT_mm"], 1)

            def proj(g, b, t):
                n = (g * B + b) * GT + t
                if isinstance(g, int) and g == 0 and b == 0 and t < 2:
                    pass
                else:
                    pe.wait_ge(s["taps"], (n - 1) * 3)
                if b == 0:
                    pe.wait_ge(s["w_split"], (g * GT + t) * 2 + 2)
                for kt in range(KT):
                    i = split_mm(ps[:, t % 2, :], wg_hi[:, t, kt, :], wg_lo[:, t, kt, :],
                                 ht_hi[:, kt, b * L:(b + 1) * L], ht_lo[:, kt, b * L:(b + 1) * L],
                                 kt == 0, kt == KT - 1)
                i.then_inc(s["proj"], 1)

            def b_transposes(q, b, p, first):
                pe.wait_ge(s["taps"], 12 * q + 3 * (p + 1))
                if not first or p:
                    pe.wait_ge(s["bt_ev"], 2 * q + p)
                for c in range(CH - 1):
                    i = nc.tensor.transpose(ps[:, 6, c * P:(c + 1) * P],
                                            acc[:, b % 2, p, c * P:(c + 1) * P], ident)
                i.then_inc(s["bt"], 1)

            def running_sums(g, q, b, j, first):
                if not first or j >= 2:
                    pe.wait_ge(s["diff_done"], 4 * q + j - 1)
                mm(ps[:, 4 + j % 2, :], sel[:, bass.ds(g * JH + j, 1), :].rearrange("p a m -> p (a m)"),
                   pT[:, b * L:(b + 1) * L], start=True, stop=True).then_inc(s["csb"], 1)

            def scores(q, b, p, first):
                pe.wait_ge(s["taps"], 12 * q + 3 * (3 + p))
                if not first or p:
                    pe.wait_ge(s["mixed"], 4 * q + 2 * p)
                for c in range(CH):
                    for a in range(2):
                        i = mm(ps[:, 2 + a, c * P:(c + 1) * P],
                               acc[NS * a:NS * (a + 1), b % 2, p, c * P:(c + 1) * P],
                               acc[NS * a:NS * (a + 1), b % 2, 2 + p, c * P:(c + 1) * P],
                               start=True, stop=True)
                        if c == CH - 1:
                            i.then_inc(s["score"], 1)

            def states(q, b):
                pe.wait_ge(s["bt_ev"], 2 * q + 2)
                pe.wait_ge(s["xds_done"], 3 * q + 3)
                for p in range(2):
                    for c in range(CH - 1):
                        n = CH - 1 - c
                        o = ps[:, 6, 3 * P + p * 48 + c * 16:3 * P + (p + 1) * 48]
                        i = mm(o, b_tok[:, p, c * P:(c + 1) * P],
                               xds[:, b % 2, V0[c]:V0[c] + n, 16 * p:16 * (p + 1)],
                               start=(c == 0), stop=(c == CH - 2))
                i.then_inc(s["state"], 1)

            def inter(q, b, first):
                pe.wait_ge(s["st_copy"], 2 * q + 2)
                if not first:
                    pe.wait_ge(s["yoff_done"], q)
                    pe.wait_ge(s["y_mid"], q)
                for c in range(1, CH):
                    for p in range(2):
                        i = mm(ps[GC:2 * GC, 7, c * P:(c + 1) * P], st_sb[:, p, c - 1, :],
                               acc[:, b % 2, 2 + p, c * P:(c + 1) * P], start=(p == 0), stop=(p == 1))
                i.then_inc(s["inter"], 1)

            def intra(q, b):
                pe.wait_ge(s["xs_done"], q + 1)
                pe.wait_ge(s["mixed"], 4 * q + 4)
                for c in range(CH):
                    for j in range(JH):
                        k = j * P + c * GC
                        i = mm(ps[0:GC, 7, c * P:(c + 1) * P], xs[:, b % 2, k:k + GC],
                               mix[:, j, c * P:(c + 1) * P], start=(j == 0), stop=(j == JH - 1))
                i.then_inc(s["intra"], 1)

            def y_transposes(q):
                pe.wait_ge(s["yt_ev"], 2 * q + 2)
                pe.sem_inc(s["pe_waits"], 1)
                for c in range(CH):
                    rows = 2 * GC if c else GC
                    i = nc.tensor.transpose(ps[:, 7, c * 2 * GC:c * 2 * GC + rows],
                                            yt_sb[0:rows, c * P:(c + 1) * P], cst[0:rows, 0, 0:rows])
                i.then_inc(s["y_tok"], 1)

            def step(g, b, gq=None, gr=None):
                bq, br = (b - 1) % B, (b - 2) % B
                q = gq * B + bq if gq is not None else None
                r = gr * B + br if gr is not None else None
                first = r is None
                project = g is not None
                if q is not None:
                    b_transposes(q, bq, 0, first)
                    running_sums(gq, q, bq, 0, first)
                    running_sums(gq, q, bq, 1, first)
                if project:
                    proj(g, b, 0)
                if r is not None:
                    intra(r, br)
                if q is not None:
                    scores(q, bq, 0, first)
                    b_transposes(q, bq, 1, first)
                if project:
                    proj(g, b, 1)
                if q is not None:
                    running_sums(gq, q, bq, 2, first)
                    running_sums(gq, q, bq, 3, first)
                if r is not None:
                    y_transposes(r)
                if q is not None:
                    scores(q, bq, 1, first)
                if project:
                    proj(g, b, 2)
                if q is not None:
                    states(q, bq)
                if project:
                    proj(g, b, 3)
                if q is not None:
                    inter(q, bq, first)

            step(0, 0)
            pe.wait_ge(s["pT_ev"], 2)
            pe.wait_ge(s["dec_done"], 1)
            pe.wait_ge(s["p_copy"], 1)
            pe.wait_ge(s["st_zero"], 1)
            pe.wait_ge(s["xs_zero"], 1)
            pe.wait_ge(s["sel_done"], 1)
            for b in range(1, B):
                step(0, b, gq=0, gr=(None if b == 1 else 0))
            with pe.Fori(1, NG) as g:
                for b in range(B):
                    step(g, b, gq=(g - 1 if b == 0 else g), gr=(g - 1 if b < 2 else g))
            step(None, 0, gq=NG - 1, gr=NG - 1)
            intra(NG * B - 1, B - 1)
            y_transposes(NG * B - 1)

            pe.wait_ge(s["bfly"], 6)
            w2_mid = stage[:, NM * D:]
            for n in range(4):
                mm(ps[:, n, :], hadamard, w2_mid[:, n * BANK:(n + 1) * BANK], start=True,
                   stop=True).then_inc(s["w2_mm"], 1)

            def gate_mms(b):
                for zt in range(2):
                    for kt in range(KT):
                        x0 = ht_hi[:, kt, bass.ds(b * L, L)]
                        x1 = ht_lo[:, kt, bass.ds(b * L, L)]
                        i = split_mm(ps[:, zt, :], wz_hi[:, zt, kt, :], wz_lo[:, zt, kt, :], x0, x1,
                                     kt == 0, kt == KT - 1)
                    i.then_inc(s["z_mm"], 1)
                pe.wait_ge(s["yv_done"], b + 1)
                for kt in range(KT):
                    for c in range(CH):
                        i = nc.tensor.transpose(ps[:, 2 + kt, c * P:(c + 1) * P], yv[:, c, kt * P:(kt + 1) * P], ident)
                    i.then_inc(s["yT_mm"], 1)

            def out_project(b):
                pe.wait_ge(s["gated"], KT * (b + 1))
                for c in range(CH):
                    for kt in range(KT):
                        i = mm(ps[:, 2 + c // 2, (c % 2) * D:(c % 2 + 1) * D], gy[:, kt, c * P:(c + 1) * P],
                               wo_sb[:, kt, :], start=(kt == 0), stop=(kt == KT - 1))
                    if c % 2:
                        i.then_inc(s["oproj"], 1)

            def norm2_transposes(b):
                pe.wait_ge(s["xn2_done"], CH * (b + 1))
                for kt in range(KT):
                    for c in range(CH):
                        i = nc.tensor.transpose(ps[:, 6 + kt, c * P:(c + 1) * P], xn2[:, c, kt * P:(kt + 1) * P], ident)
                    i.then_inc(s["lnT2"], 1)

            def up(b):
                pe.wait_ge(s["h2lo_done"], KT * (b + 1))
                pe.wait_ge(s["x1_done"], 2 * (b + 1))
                for m in range(NM):
                    if m >= 2:
                        pe.wait_ge(s["hid_done"], b * NM + m - 1)
                    for half in range(2):
                        for kt in range(KT):
                            i = split_mm(ps[:, 2 * half + m % 2, :], w13_hi[:, m, half, kt, :],
                                         w13_lo[:, m, half, kt, :], h2_hi[:, kt, :], h2_lo[:, kt, :],
                                         kt == 0, kt == KT - 1)
                    i.then_inc(s["up_mm"], 1)

            def down(b, c, first=False):
                if c == 0:
                    pe.wait_ge(s["hlo2"], NM * (b + 1))
                if not (first and c < 2):
                    pe.wait_ge(s["out_mul"], b * CH + c - 1)
                for m in range(NM):
                    i = split_mm(ps[:, 4 + c % 2, 0:D], hid_hi[:, m, c * P:(c + 1) * P], hid_lo[:, m, c * P:(c + 1) * P],
                                 w2_hi[:, m, :], w2_lo[:, m, :], m == 0, m == NM - 1)
                i.then_inc(s["down_mm"], 1)

            pe.wait_ge(s["w2_hi_done"], 4)
            pe.wait_ge(s["w2_split"], 4)
            pe.wait_ge(s["wz_split"], 2)
            gate_mms(0)
            pe.wait_ge(s["ld_wo"], 16)
            out_project(0)
            norm2_transposes(0)

            def ffn_step(b, more, first=False):
                up(b)
                if more:
                    pe.wait_ge(s["hid_done"], NM * (b + 1))
                    gate_mms(b + 1)
                down(b, 0, first)
                if more:
                    out_project(b + 1)
                down(b, 1, first)
                down(b, 2, first)
                if more:
                    norm2_transposes(b + 1)
                down(b, 3, first)

            ffn_step(0, True, first=True)
            with pe.Fori(1, B - 1) as b:
                ffn_step(b, True)
            ffn_step(B - 1, False)

        @block.scalar
        def _(act):
            af = nc.scalar.activation

            act.wait_ge(s["ld_c"], 16)
            af(c_exp[:], c_sb[:], ACT.Exp, scale=-1.0).then_inc(s["c_exp_done"], 1)

            def h_parts(b):
                act.wait_ge(s["lnT_mm"], b + 1)
                for kt in range(KT):
                    n = KT * b + kt
                    if b:
                        act.wait_ge(s["hlo_done"], n - 1)
                    af(h32[:, kt, :], ps[:, 2 + kt, :], ACT.Identity, bias=shift[:, 0, kt, b:b + 1],
                       scale=scale1[:, 0, kt, b:b + 1]).then_inc(s["h32_done"], 1)
                for kt in range(KT):
                    act.wait_ge(s["h32_done"], KT * b + kt + 1)
                    nc.scalar.copy(ht_hi[:, kt, b * L:(b + 1) * L], h32[:, kt, :]).then_inc(s["hhi_done"], 1)

            def x_tap(b):
                for xt in range(2):
                    n = 2 * b + xt
                    act.wait_ge(s["xp_mm"], n + 1)
                    w = conv_sb[:, NG * GT + xt, :]
                    af(acc[:, n // GT, n % GT, :], ps[:, xt, :], ACT.Identity, bias=w[:, TAPS:TAPS + 1],
                       scale=w[:, TAPS - 1:TAPS]).then_inc(s["xtap"], 1)

            def x_evacuate(b):
                for xt in range(2):
                    n = 2 * b + xt
                    act.wait_ge(s["xT_mm"], n + 1)
                    nc.scalar.copy(x_tok[:, b * CH:(b + 1) * CH, xt * P:(xt + 1) * P],
                                   ps[:, 4 + xt, :].rearrange("p (c m) -> p c m", c=CH)).then_inc(s["xtok_ev"], 1)

            act.wait_ge(s["mod_ev"], 2)
            act.wait_ge(s["ld_conv"], 16)
            h_parts(0)
            for b in range(B):
                if b + 1 < B:
                    h_parts(b + 1)
                if b == 0:
                    for n in range(B):
                        act.wait_ge(s["gate_mm"], n + 1)
                        if n:
                            act.wait_ge(s["gate_ev2"], n)
                        af(a_abs[:], ps[:, 4 + n, :], ACT.Abs).then_inc(s["gate_abs"], 1)
                x_tap(b)
                if b:
                    x_evacuate(b - 1)
            x_evacuate(B - 1)

            act.wait_ge(s["a_mm"], 1)
            act.wait_ge(s["gate_ev"], 1)
            af(a_abs[:], ps[:, 6, :], ACT.Abs).then_inc(s["abs_done"], 1)
            act.wait_ge(s["abs_done"], 1)
            af(a_exp[:], a_abs[:], ACT.Exp, scale=-1.0).then_inc(s["aexp_done"], 1)
            act.wait_ge(s["aexp_done"], 1)
            af(a_exp[:], a_exp[:], ACT.Ln, bias=1.0).then_inc(s["aln_done"], 1)
            act.wait_ge(s["p_copy"], 1)
            af(e_tok[:].rearrange("p t h -> p (t h)"), ps[:, 7, :], ACT.Exp, scale=-1.0).then_inc(s["e_done"], 1)
            act.wait_ge(s["dk_mm"], 1)
            for k in range(2):
                i = af(dec[:, 3 * k:3 * k + 3, :, :].rearrange("p v b h -> p (v b h)"), ps[:, 4 + k, 0:3 * B * NH],
                       ACT.Exp, scale=-1.0)
            i.then_inc(s["dec_done"], 1)
            act.wait_ge(s["pT_mm"], 1)
            for k in range(2):
                nc.scalar.copy(pT[:, k * 1024:(k + 1) * 1024],
                               ps[0:3 * NH, 2 + k, :].bitcast(BF16)).then_inc(s["pT_ev"], 1)

            def last_tap(g, b, t):
                n = (g * B + b) * GT + t
                act.wait_ge(s["proj"], n + 1)
                af(acc[:, b % 2, t, :], ps[:, t % 2, :], ACT.Identity, bias=cw_act[:, t, 1:2],
                   scale=cw_act[:, t, 0:1]).then_inc(s["tap0"], 1)

            def b_evacuate(q, p):
                act.wait_ge(s["bt"], 2 * q + p + 1)
                nc.scalar.copy(b_tok[:, p, :], ps[:, 6, 0:3 * P]).then_inc(s["bt_ev"], 1)

            def decays(q, b, j, first):
                act.wait_ge(s["csb"], 4 * q + j + 1)
                if not first:
                    act.wait_ge(s["mixed"], 4 * q + j - 3)
                for c in range(CH):
                    i = af(decay[:, j, c * P:(c + 1) * P], ps[:, 4 + j % 2, c * P:(c + 1) * P], ACT.Relu,
                           bias=p_slot[:, b * CH + c, j:j + 1])
                i.then_inc(s["diff_done"], 1)
                act.wait_ge(s["diff_done"], 4 * q + j + 1)
                af(decay[:, j, :], decay[:, j, :], ACT.Exp, scale=-1.0).then_inc(s["exp_done"], 1)

            def inter_evacuate(r, start):
                act.wait_ge(s["inter"], r + 1)
                if not start:
                    act.wait_ge(s["y_tok"], r)
                nc.scalar.copy(yt_sb[GC:2 * GC, P:], ps[GC:2 * GC, 7, P:]).then_inc(s["yt_ev"], 1)

            def intra_evacuate(r):
                act.wait_ge(s["intra"], r + 1)
                nc.scalar.copy(yt_sb[0:GC, :], ps[0:GC, 7, :]).then_inc(s["yt_ev"], 1)

            def step(g, b, attend=True, project=True, gq=None, gr=None, first=False):
                bq = (b - 1) % B
                q = gq * B + bq if attend else None
                first_r = isinstance(gr, int) and gr == 0 and b == 2
                if project and b == 0:
                    if attend:
                        act.wait_ge(s["tap0"], g * (GT * B))
                    nc.scalar.copy(cw_act[:], conv_sb[:, bass.ds(g * GT, GT), TAPS - 1:TAPS + 1]).then_inc(s["cwa"], 1)
                if project and b == 1:
                    act.wait_ge(s["exp_done"], g * 4 * B) if not (isinstance(g, int) and g == 0) else None
                    nc.scalar.mul(p_slot[:], p_tok[:, :, bass.ds(g * JH, JH)], -1.0).then_inc(s["p_sl"], 1)
                    act.wait_ge(s["p_sl"], g + 1)
                if attend:
                    b_evacuate(q, 0)
                    decays(q, bq, 0, first)
                if gr is not None:
                    inter_evacuate(gr * B + (b - 2) % B, first_r)
                if project:
                    if b == 0:
                        act.wait_ge(s["cwa"], g + 1)
                    last_tap(g, b, 0)
                if attend:
                    decays(q, bq, 1, first)
                if gr is not None:
                    intra_evacuate(gr * B + (b - 2) % B)
                if attend:
                    b_evacuate(q, 1)
                if project:
                    last_tap(g, b, 1)
                if attend:
                    decays(q, bq, 2, first)
                    decays(q, bq, 3, first)
                if project:
                    last_tap(g, b, 2)
                    last_tap(g, b, 3)

            act.wait_ge(s["xT_mm"], 2 * B)
            step(0, 0, attend=False)
            for b in range(1, B):
                step(0, b, gq=0, gr=(None if b == 1 else 0), first=(b == 1))
            with act.Fori(1, NG) as g:
                for b in range(B):
                    step(g, b, gq=(g - 1 if b == 0 else g), gr=(g - 1 if b < 2 else g))
            step(None, 0, gq=NG - 1, gr=NG - 1, project=False)
            inter_evacuate(NG * B - 1, False)
            intra_evacuate(NG * B - 1)

            for n in range(4):
                act.wait_ge(s["w2_mm"], n + 1)
                nc.scalar.copy(w2_hi[:, 2 * n:2 * n + 2, :].rearrange("p m d -> p (m d)"),
                               ps[:, n, :]).then_inc(s["w2_hi_done"], 1)

            def silu_gate(b):
                for zt in range(2):
                    act.wait_ge(s["z_mm"], 2 * b + zt + 1)
                    af(sz[:, zt, :], ps[:, zt, :], ACT.Silu, bias=zb_sb[:, zt:zt + 1]).then_inc(s["silu_z"], 1)

            def h2_parts(b):
                for kt in range(KT):
                    act.wait_ge(s["lnT2"], KT * b + kt + 1)
                    af(h32b[:, kt, :], ps[:, 6 + kt, :], ACT.Identity, bias=shift[:, 1, kt, bass.ds(b, 1)],
                       scale=scale1[:, 1, kt, bass.ds(b, 1)]).then_inc(s["h32b_done"], 1)
                for kt in range(KT):
                    act.wait_ge(s["h32b_done"], KT * b + kt + 1)
                    nc.scalar.copy(h2_hi[:, kt, :], h32b[:, kt, :]).then_inc(s["h2hi_done"], 1)

            def hidden(b, first):
                for m in range(NM):
                    n = b * NM + m
                    act.wait_ge(s["up_mm"], n + 1)
                    if not (first and m < 2):
                        act.wait_ge(s["hid_done"], n - 1)
                    af(silu_sb[:, m % 2, :], ps[:, m % 2, :], ACT.Silu).then_inc(s["silu_done"], 1)
                    act.wait_ge(s["hid_done"], n + 1)
                    if m == 0 and not first:
                        act.wait_ge(s["down_mm"], b * CH)
                    nc.scalar.copy(hid_hi[:, m, :], hid[:, m % 2, :]).then_inc(s["hhi2"], 1)

            act.wait_ge(s["ld_zb"], 16)
            silu_gate(0)
            h2_parts(0)
            hidden(0, True)
            silu_gate(1)
            h2_parts(1)
            with act.Fori(1, B - 1) as b:
                hidden(b, False)
                silu_gate(b + 1)
                h2_parts(b + 1)
            hidden(B - 1, False)

        @block.vector
        def _(dve):
            ts = nc.vector.tensor_scalar
            tt = nc.vector.tensor_tensor
            stt = nc.vector.scalar_tensor_tensor

            dve.wait_ge(s["c_exp_done"], 1)
            ts(c_exp[:], c_exp[:], 1.0, None, ALU.add).then_inc(s["c_one"], 1)
            dve.wait_ge(s["c_one"], 1)
            nc.vector.reciprocal(c_exp[:], c_exp[:]).then_inc(s["c_rec"], 1)
            dve.wait_ge(s["c_rec"], 1)
            tt(c_silu[:], c_sb[:], c_exp[:], ALU.mult).then_inc(s["c_silu_done"], 1)
            dve.wait_ge(s["c_silu_done"], 1)
            for kt in range(KT):
                for b in range(B):
                    nc.vector.tensor_copy(c_rows[:, kt, b, :],
                                          c_silu[:, kt, b:b + 1].to_broadcast([P, P])).then_inc(s["c_rows_done"], 1)
            nc.vector.memset(st_sb[:], 0.0).then_inc(s["st_zero"], 1)
            nc.vector.memset(xs[:], 0.0).then_inc(s["xs_zero"], 1)

            def normalise(src, dst, n, names):
                st, ag, ep, rs, done = names
                for c in range(CH):
                    nc.vector.bn_stats(stats[:, c, :], src[:, c, :]).then_inc(s[st], 1)
                for c in range(CH):
                    dve.wait_ge(s[st], n * CH + c + 1)
                    dve.sem_inc(s["dve_waits"], 1)
                    nc.vector.bn_aggr(meanvar[:, c, :], stats[:, c, :]).then_inc(s[ag], 1)
                dve.wait_ge(s[ag], n * CH + CH)
                ts(vareps[:], meanvar[:, :, 1], EPS, None, ALU.add).then_inc(s[ep], 1)
                dve.wait_ge(s[rs], n + 1)
                for c in range(CH):
                    ts(dst[:, c, :], src[:, c, :], meanvar[:, c, 0:1], rstd[:, c:c + 1], ALU.subtract,
                       ALU.mult).then_inc(s[done], 1)

            def norm1(b):
                dve.wait_ge(s[f"ld_u{b}"], 16)
                if b >= 2:
                    dve.wait_ge(s["lnT_mm"], b - 1)
                normalise(u_sb[:, b * CH:(b + 1) * CH, :], xn[:, b % 2], b, ("bnst", "bnag", "eps1", "rs", "xn_done"))

            def h_low(b):
                for kt in range(KT):
                    dve.wait_ge(s["hhi_done"], KT * b + kt + 1)
                    tt(ht_lo[:, kt, b * L:(b + 1) * L], h32[:, kt, :], ht_hi[:, kt, b * L:(b + 1) * L].bitcast(F32),
                       ALU.subtract).then_inc(s["hlo_done"], 1)

            def taps(a, bank, w, name, n):
                for k in range(TAPS - 1):
                    d = k + 1
                    if k:
                        dve.wait_ge(s[name], n + k)
                    stt(a[:, d:], ps[:, bank, 0:L - d], w[:, TAPS - 1 - d:TAPS - d], a[:, d:], ALU.mult,
                        ALU.add).then_inc(s[name], 1)

            def x_taps(b):
                for xt in range(2):
                    n = 2 * b + xt
                    dve.wait_ge(s["xtap"], n + 1)
                    taps(acc[:, n // GT, n % GT, :], xt, conv_sb[:, NG * GT + xt, :], "xtaps", 3 * n)

            norm1(0)
            dve.wait_ge(s["mod_mm"], 1)
            mod = ps[:, 0, 0:4 * KT * B].rearrange("p (n k m b) -> p n k m b", n=2, k=2, m=KT)
            nc.vector.tensor_copy(shift[:], mod[:, :, 0]).then_inc(s["mod_ev"], 1)
            ts(scale1[:], mod[:, :, 1], 1.0, None, ALU.add).then_inc(s["mod_ev"], 1)
            dve.wait_ge(s["ld_wx"], 16)
            nc.vector.tensor_copy(wx_hi[:], wx_raw[:]).then_inc(s["wx_split"], 1)
            dve.wait_ge(s["wx_split"], 1)
            tt(wx_lo[:], wx_raw[:], wx_hi[:].bitcast(F32), ALU.subtract).then_inc(s["wx_split"], 1)
            dve.wait_ge(s["ld_wa"], 16)
            nc.vector.tensor_copy(wa_hi[:], wa_raw[:]).then_inc(s["wa_split"], 1)
            dve.wait_ge(s["wa_split"], 1)
            tt(wa_lo[:], wa_raw[:], wa_hi[:].bitcast(F32), ALU.subtract).then_inc(s["wa_split"], 1)
            norm1(1)
            h_low(0)
            for b in range(B):
                dve.wait_ge(s["gate_mm"], b + 1)
                gp = ps[:, 4 + b, :]
                gt = gates[:, b].rearrange("p k d -> p (k d)")
                dve.wait_ge(s["gate_abs"], b + 1)
                ts(gt, gp, 0.0, 2.0, ALU.is_ge, ALU.mult).then_inc(s["gate_sign"], 1)
                ts(a_abs[:], a_abs[:], 0.25, None, ALU.max).then_inc(s["gate_sign"], 1)
                dve.wait_ge(s["gate_sign"], 2 * b + 2)
                stt(gt, gt, -1.0, a_abs[:], ALU.add, ALU.mult).then_inc(s["gate_ev2"], 1)
                dve.wait_ge(s["gate_ev2"], b + 1)
            nc.vector.tensor_copy(ident_bf[:], ident).then_inc(s["gate_ev"], 1)
            for b in range(B):
                if b + 2 < B:
                    norm1(b + 2)
                if b + 1 < B:
                    h_low(b + 1)
                dve.wait_ge(s["ld_conv"], 16)
                x_taps(b)

            dve.wait_ge(s["aln_done"], 1)
            stt(sp_a[:].rearrange("p b c h -> p (b c h)"), ps[:, 6, :], 0.0, a_exp[:], ALU.max,
                ALU.add).then_inc(s["sp_done"], 1)
            dve.wait_ge(s["ptok_mm"], 1)
            nc.vector.tensor_copy(p_tok[:].rearrange("p t h -> p (t h)"), ps[:, 7, :]).then_inc(s["p_copy"], 1)
            dve.wait_ge(s["p_copy"], 1)
            rest = a_abs[:].rearrange("p (t h) -> p t h", h=NH)
            nc.vector.tensor_copy(parts[:, :, 0, :], p_tok[:]).then_inc(s["part_step"], 1)
            dve.wait_ge(s["part_step"], 1)
            tt(rest, p_tok[:], parts[:, :, 0, :], ALU.subtract).then_inc(s["part_step"], 1)
            dve.wait_ge(s["part_step"], 2)
            nc.vector.tensor_copy(parts[:, :, 1, :], rest).then_inc(s["part_step"], 1)
            dve.wait_ge(s["part_step"], 3)
            tt(parts[:, :, 2, :], rest, parts[:, :, 1, :], ALU.subtract).then_inc(s["parts_done"], 1)

            def mix_head(q, j, first):
                dve.wait_ge(s["score"], 4 * q + j + 1)
                dve.wait_ge(s["masked"], 4 * q + j + 1)
                if not first:
                    dve.wait_ge(s["intra"], q)
                tt(mix[:, j, :], ps[:, 2 + j % 2, :], decay[:, j, :], ALU.mult).then_inc(s["mixed"], 1)

            def conv_tile(g, b, t):
                n = (g * B + b) * GT + t
                dve.wait_ge(s["tap0"], n + 1)
                taps(acc[:, b % 2, t, :], t % 2, cw_dve[:, t, :], "taps", 3 * n)

            def copy_states(q, first):
                dve.wait_ge(s["state"], q + 1)
                for a in range(2):
                    src = ps[NS * a:NS * (a + 1), 6, 3 * P:3 * P + 96].rearrange("n (p t w) -> n p t w", p=2, t=3)
                    for p in range(2):
                        k = 2 * HD * p + HD * a
                        i = nc.vector.tensor_copy(st_sb[NS * a:NS * (a + 1), p, :, k:k + HD],
                                                  src[:, p, :, HD * a:HD * (a + 1)])
                    i.then_inc(s["st_copy"], 1)

            def y_combine(gq, q, b):
                dve.wait_ge(s["y_tok"], q + 1)
                dve.wait_ge(s["xd_done"], q + 1)
                y = ps[:, 7, 0:2 * P].rearrange("p (c k w) -> p c k w", c=CH, k=2)
                o = y[:, 1:, 1].rearrange("p c (j e) -> p c j e", j=JH)
                e = e_tok[:, b * CH + 1:(b + 1) * CH, bass.ds(gq * JH, JH)].unsqueeze(3).to_broadcast([P, 3, JH, HD])
                tt(y_off[:].rearrange("p c (j e) -> p c j e", j=JH), o, e, ALU.mult).then_inc(s["yoff_done"], 1)
                x = x_tok[:, b * CH:(b + 1) * CH, bass.ds(gq * GC, GC)]
                tt(x, y[:, :, 0], x, ALU.add).then_inc(s["y_mid"], 1)
                x = x_tok[:, b * CH + 1:(b + 1) * CH, bass.ds(gq * GC, GC)]
                dve.wait_ge(s["yoff_done"], q + 1)
                dve.wait_ge(s["y_mid"], q + 1)
                tt(x, x, y_off[:], ALU.add).then_inc(s["y_done"], 1)

            def step(g, b, attend=True, project=True, gq=None, gr=None, first=False):
                bq = (b - 1) % B
                q = gq * B + bq if attend else None
                if project and b == 0:
                    if attend:
                        dve.wait_ge(s["taps"], g * (3 * GT * B))
                    nc.vector.tensor_copy(cw_dve[:], conv_sb[:, bass.ds(g * GT, GT), 0:3]).then_inc(s["cwd"], 1)
                if project:
                    if b == 0:
                        dve.wait_ge(s["cwd"], g + 1)
                    conv_tile(g, b, 0)
                if attend:
                    mix_head(q, 0, first)
                    mix_head(q, 1, first)
                if project:
                    conv_tile(g, b, 1)
                if gr is not None:
                    y_combine(gr, gr * B + (b - 2) % B, (b - 2) % B)
                if attend:
                    mix_head(q, 2, first)
                    mix_head(q, 3, first)
                    copy_states(q, first)
                if project:
                    conv_tile(g, b, 2)
                    conv_tile(g, b, 3)

            dve.wait_ge(s["e_done"], 1)
            step(0, 0, attend=False)
            for b in range(1, B):
                step(0, b, gq=0, gr=(None if b == 1 else 0), first=(b == 1))
            with dve.Fori(1, NG) as g:
                for b in range(B):
                    step(g, b, gq=(g - 1 if b == 0 else g), gr=(g - 1 if b < 2 else g))
            step(None, 0, gq=NG - 1, gr=NG - 1, project=False)
            y_combine(NG - 1, NG * B - 1, B - 1)

            for n in range(4):
                dve.wait_ge(s["w2_hi_done"], n + 1)
                w = w2_lo[:, 2 * n:2 * n + 2, :].rearrange("p m d -> p (m d)")
                h = w2_hi[:, 2 * n:2 * n + 2, :].rearrange("p m d -> p (m d)")
                tt(w, ps[:, n, :], h.bitcast(F32), ALU.subtract).then_inc(s["w2_split"], 1)

            def gate_and_norm(b, first=False):
                for kt in range(KT):
                    dve.wait_ge(s["yT_mm"], KT * b + kt + 1)
                    dve.wait_ge(s["silu_z"], KT * b + kt + 1)
                    tt(gy[:, kt, :], ps[:, 2 + kt, :], sz[:, kt, :], ALU.mult).then_inc(s["gated"], 1)
                dve.wait_ge(s["ld_res"], (b + 1) * 16)
                ga = gates[:, bass.ds(b, 1), 0, :].to_broadcast([P, 2, D])
                for h in range(2):
                    n = 2 * b + h
                    dve.wait_ge(s["oproj"], n + 1)
                    o = ps[:, 2 + h, :].rearrange("p (c d) -> p c d", c=2)
                    if not first:
                        dve.wait_ge(s["x1_done"], n - 1)
                    tt(ga_out[:, h], o, ga, ALU.mult).then_inc(s["res_mul"], 1)
                    dve.wait_ge(s["res_mul"], n + 1)
                    tt(x_tok[:, bass.ds(b * CH + 2 * h, 2), :], ga_out[:, h], u2[:, 2 * h:2 * h + 2, :],
                       ALU.add).then_inc(s["x1_done"], 1)
                dve.wait_ge(s["ld_c"], 16)
                if not first:
                    dve.wait_ge(s["lnT2"], KT * b)
                dve.wait_ge(s["x1_done"], 2 * b + 2)
                normalise(x_tok[:, bass.ds(b * CH, CH), :], xn2[:], b, ("bn2", "ag2", "eps2", "rs2", "xn2_done"))

            def h2_low(b):
                for kt in range(KT):
                    dve.wait_ge(s["h2hi_done"], KT * b + kt + 1)
                    tt(h2_lo[:, kt, :], h32b[:, kt, :], h2_hi[:, kt, :].bitcast(F32),
                       ALU.subtract).then_inc(s["h2lo_done"], 1)

            def hidden(b, first):
                for m in range(NM):
                    n = b * NM + m
                    dve.wait_ge(s["silu_done"], n + 1)
                    if not (first and m < 2):
                        dve.wait_ge(s["hlo2"], n - 1)
                    tt(hid[:, m % 2, :], ps[:, 2 + m % 2, :], silu_sb[:, m % 2, :], ALU.mult).then_inc(s["hid_done"], 1)
                    if m:
                        hidden_low(n - 1, m - 1)
                hidden_low(b * NM + NM - 1, NM - 1)

            def hidden_low(n, m):
                dve.wait_ge(s["hhi2"], n + 1)
                tt(hid_lo[:, m, :], hid[:, m % 2, :], hid_hi[:, m, :].bitcast(F32), ALU.subtract).then_inc(s["hlo2"], 1)

            def residual(b, c, first):
                n = b * CH + c
                dve.wait_ge(s["down_mm"], n + 1)
                x = x_tok[:, bass.ds(n, 1), :]
                t = gb_out[:, c % 2]
                if not (first and c < 2):
                    dve.wait_ge(s["x2_done"], n - 1)
                tt(t, ps[:, 4 + c % 2, 0:D].unsqueeze(1), gates[:, bass.ds(b, 1), 1, :], ALU.mult).then_inc(s["out_mul"], 1)
                dve.wait_ge(s["out_mul"], n + 1)
                tt(x, x, t, ALU.add).then_inc(s["x2_done"], 1)

            gate_and_norm(0, first=True)
            h2_low(0)

            def ffn_step(b, more, first=False):
                hidden(b, first)
                if more:
                    gate_and_norm(b + 1)
                residual(b, 0, first)
                residual(b, 1, first)
                if more:
                    h2_low(b + 1)
                residual(b, 2, first)
                residual(b, 3, first)

            ffn_step(0, True, first=True)
            with dve.Fori(1, B - 1) as b:
                ffn_step(b, True)
            ffn_step(B - 1, False)

        @block.gpsimd
        def _(pool):
            gp = nc.gpsimd

            def await_unit(name, value):
                pool.wait_ge(s[name], value)
                pool.sem_inc(s["pool_waits"], 1)

            gp.memset(minus_half[:], -0.5).then_inc(s["half_set"], 1)
            pool.wait_ge(s["half_set"], 1)

            def split_tile(g, t):
                n = (g * GT + t) * 2
                gp.tensor_copy(wg_hi[:, t], wg_raw[:, t]).then_inc(s["w_split"], 1)
                await_unit("w_split", n + 1)
                gp.tensor_tensor(wg_lo[:, t], wg_raw[:, t], wg_hi[:, t].bitcast(F32), ALU.subtract).then_inc(s["w_split"], 1)

            def inverse_root(n, eps_name, name):
                await_unit(eps_name, n + 1)
                gp.tensor_tensor(rstd[:], vareps[:], minus_half[:], ALU.pow).then_inc(s[name], 1)

            for b in range(B):
                inverse_root(b, "eps1", "rs")
            pool.wait_ge(s["ld_wg"], 16)
            for t in range(GT):
                split_tile(0, t)
            pool.wait_ge(s["ld_hot"], 16)
            gp.tensor_copy(sel[:], hot_sb[:].unsqueeze(2).to_broadcast([3 * NH, NH, P])).then_inc(s["sel_done"], 1)
            pool.wait_ge(s["ld_wz"], 16)
            gp.tensor_copy(wz_hi[:], wz_raw[:]).then_inc(s["wz_split"], 1)
            pool.wait_ge(s["wz_split"], 1)
            gp.tensor_tensor(wz_lo[:], wz_raw[:], wz_hi[:].bitcast(F32), ALU.subtract).then_inc(s["wz_split"], 1)
            pool.wait_ge(s["ld_d"], 16)

            def scale_x(gq, q, b, first, second):
                if not first:
                    await_unit("state", q)
                for c in range(CH - 1):
                    n = CH - 1 - c
                    xc = x_tok[:, b * CH + c:b * CH + c + 1, bass.ds(gq * GC, GC)]
                    x4 = xc.rearrange("p t (j e) -> p t j e", j=JH).to_broadcast([P, n, JH, HD])
                    d4 = dec[:, V0[c]:V0[c] + n, b, bass.ds(gq * JH, JH)].unsqueeze(3).to_broadcast([P, n, JH, HD])
                    o4 = xds[:, b % 2, V0[c]:V0[c] + n, :].rearrange("p t (j e) -> p t j e", j=JH)
                    gp.tensor_tensor(o4, x4, d4, ALU.mult).then_inc(s["xds_done"], 1)
                if not (first or second):
                    await_unit("intra", q - 1)
                x = x_tok[:, b * CH:(b + 1) * CH, bass.ds(gq * GC, GC)]
                own = xs[:, b % 2].rearrange("p (j n) -> p j n", j=JH)[:, :, 0:P]
                own = own.rearrange("p j (c w) -> p c j w", c=CH)[:, :, :, 0:HD]
                gp.tensor_copy(own, x.rearrange("p c (j e) -> p c j e", j=JH)).then_inc(s["xs_done"], 1)
                await_unit("xs_done", q + 1)
                await_unit("xds_done", 3 * q + 3)
                x4 = x.rearrange("p c (j e) -> p c j e", j=JH)
                d4 = d_sb[:, bass.ds(gq * JH, JH)].unsqueeze(1).unsqueeze(3).to_broadcast([P, CH, JH, HD])
                gp.tensor_tensor(x4, x4, d4, ALU.mult).then_inc(s["xd_done"], 1)

            def mask(q, j):
                await_unit("exp_done", 4 * q + j + 1)
                v = decay[:, j, :].rearrange("p (c l) -> p c l", c=CH)
                gp.affine_select(out=v, in_=v, compare_op=ALU.is_ge, fill=0.0, base=0, pattern=[[0, CH], [1, P]],
                                 channel_multiplier=-1).then_inc(s["masked"], 1)

            def step(g, b, gq, first=False, split=False):
                bq = (b - 1) % B
                q = gq * B + bq
                scale_x(gq, q, bq, first, isinstance(q, int) and q == 1)
                mask(q, 0)
                mask(q, 1)
                if split:
                    await_unit("ld_wg", (g + 2) * 16)
                    for t in range(2):
                        await_unit("proj", (g * B + B - 1) * GT + t + 1)
                        split_tile(g + 1, t)
                mask(q, 2)
                mask(q, 3)
                if split:
                    for t in range(2, 4):
                        await_unit("proj", (g * B + B - 1) * GT + t + 1)
                        split_tile(g + 1, t)

            pool.wait_ge(s["dec_done"], 1)
            pool.wait_ge(s["xs_zero"], 1)
            pool.wait_ge(s["xtok_ev"], 2 * B)
            w13r = stage[:].rearrange("p (m h k n) -> p m h k n", m=NM, h=2, k=KT)
            for b in range(1, B):
                step(0, b, 0, first=(b == 1), split=(b == B - 1))
                if b == 1:
                    pool.wait_ge(s["ld_w13"], 16)
                    pool.wait_ge(s["xp_mm"], 2 * B)
                    pool.wait_ge(s["hlo_done"], KT * B)
                    pool.wait_ge(s["gate_mm"], B)
                for m in range(3 * (b - 1), min(3 * b, NM)):
                    gp.tensor_copy(w13_hi[:, m], w13r[:, m]).then_inc(s["w13_hi_done"], 1)
                    pool.wait_ge(s["w13_hi_done"], m + 1)
                    gp.tensor_tensor(w13_lo[:, m], w13r[:, m], w13_hi[:, m].bitcast(F32),
                                     ALU.subtract).then_inc(s["w13_split"], 1)
            with pool.Fori(1, NG - 1) as g:
                for b in range(B):
                    step(g, b, (g - 1 if b == 0 else g), split=(b == B - 1))
            half = [stage[:, 0:NM * D], stage[:, NM * D:]]

            def butterfly(k):
                w = 1 << k
                src = half[k % 2].rearrange("p (n e w d) -> p n e (w d)", e=2, w=w, d=D)
                dst = half[1 - k % 2].rearrange("p (n e w d) -> p n e (w d)", e=2, w=w, d=D)
                if k:
                    pool.wait_ge(s["bfly"], 2 * k)
                gp.tensor_tensor(dst[:, :, 0], src[:, :, 0], src[:, :, 1], ALU.add).then_inc(s["bfly"], 1)
                gp.tensor_tensor(dst[:, :, 1], src[:, :, 0], src[:, :, 1], ALU.subtract).then_inc(s["bfly"], 1)

            for b in range(B):
                step(NG - 1, b, NG - 2 if b == 0 else NG - 1)
                if b == 0:
                    pool.wait_ge(s["ld_w2"], 16)
                if b < 3:
                    butterfly(b)
            step(None, 0, NG - 1)

            def y_values(b):
                gp.tensor_copy(yv[:], x_tok[:, bass.ds(b * CH, CH), :]).then_inc(s["yv_done"], 1)

            pool.wait_ge(s["y_done"], NG * B)
            y_values(0)
            inverse_root(0, "eps2", "rs2")
            with pool.Fori(1, B) as b:
                await_unit("yT_mm", KT * b)
                y_values(b)
                inverse_root(b, "eps2", "rs2")


def _layout(i):
    import numpy as np

    f = {k: np.asarray(v) for k, v in i.items()}
    w_in = f["L0_attn_W_in"]
    conv_w = f["L0_attn_conv_w"][:, 0, :]
    nb = NH * NS
    k_major = lambda w: w.T.reshape(KT, P, -1).transpose(1, 0, 2)

    def tiles(w):
        return k_major(w).reshape(P, KT, -1, P).transpose(0, 2, 1, 3)

    bt = tiles(w_in[D:D + nb]).reshape(P, NG, 2, KT, P)
    ct = tiles(w_in[D + nb:D + 2 * nb]).reshape(P, NG, 2, KT, P)
    taps = np.concatenate([conv_w, f["L0_attn_conv_b"][:, None]], axis=1)
    xc = taps[:D].reshape(2, P, TAPS + 1)
    bc = taps[D:D + nb].reshape(NG, 2, P, TAPS + 1)
    cc = taps[D + nb:].reshape(NG, 2, P, TAPS + 1)
    groups = np.concatenate([bc, cc], axis=1).reshape(NG * GT, P, TAPS + 1)
    w1, w3 = (tiles(f[n]) for n in ("L0_ffn_W1", "L0_ffn_W3"))
    n = np.arange(P)
    had = np.array([[1.0]])
    while len(had) < P:
        had = np.block([[had, had], [had, -had]])
    consts = np.stack([np.eye(P), n[:, None] <= n[None, :], n[:, None] > n[None, :], np.ones((P, P)),
                       had / np.sqrt(HID)], axis=1).astype(np.float32)
    return {
        "u": f["L0_attn_u"].reshape(B * L, D),
        "w_bc": np.concatenate([bt, ct], axis=2).transpose(1, 0, 2, 3, 4),
        "w_x": tiles(w_in[:D]),
        "w_a": k_major(w_in[2 * D + 2 * nb:]),
        "w_z": tiles(w_in[D + 2 * nb:2 * D + 2 * nb]),
        "conv": np.concatenate([groups, xc], axis=0).transpose(1, 0, 2),
        "d_rows": np.broadcast_to(f["L0_attn_D"], (P, NH)),
        "z_bias": f["L0_attn_z_bias"].reshape(2, P).T,
        "w_out": k_major(f["L0_attn_W_out"]),
        "w13": np.stack([w1, w3], axis=2).reshape(P, -1),
        "w2": f["L0_ffn_W2"].T.reshape(NM, P, D).transpose(1, 0, 2).reshape(P, -1),
        "c_t": f["L0_c"].T.reshape(KT, P, B).transpose(1, 0, 2),
        "wmod": f["L0_wmod"].reshape(KT, P, 6 * D).transpose(1, 0, 2),
        "consts": consts,
        "head_hot": np.tile(np.eye(NH, dtype=np.float32), (3, 1)),
    }


def kernel(**inputs):
    import numpy as _np
    import concourse.bacc as _bacc
    from concourse import mybir as _mybir
    from concourse.bass_utils import run_bass_kernel_spmd as _run

    nc = _bacc.Bacc("TRN2", target_bir_lowering=False, num_devices=1)
    arrays, args = {}, []
    for name, a in _layout(inputs).items():
        a = _np.ascontiguousarray(a)
        arrays[f"in_{name}"] = a
        args.append(nc.dram_tensor(f"in_{name}", a.shape, _mybir.dt.from_np(a.dtype), kind="ExternalInput").ap())
    args.append(nc.dram_tensor("out_0", (B * L, D), _mybir.dt.float32, kind="ExternalOutput").ap())
    adaln_ssm_ffn_kernel(nc, *args)
    r = _run(nc, [arrays], core_ids=[0])
    return r.results[0]["out_0"].reshape(B, L, D)
```

```python
from contextlib import ExitStack

import concourse.bass as bass
from concourse import mybir

F32 = mybir.dt.float32
F32R = mybir.dt.float32r
BF16 = mybir.dt.bfloat16
ALU = mybir.AluOpType
ACT = mybir.ActivationFunctionType

P = 128
B, L, D = 4, 512, 256
NH, HD, NS = 32, 8, 64
HID = 1024
TAPS = 4
KT = D // P
CH = L // P
TT = B * CH
JH = 4
NG = NH // JH
GT = 4
GC = JH * HD
NM = HID // P
BANK = 512
EPS = 1e-5
SLOTS = 2
V0 = [0, 3, 5]
NV = 6


def adaln_ssm_ffn_kernel(nc, u, w_bc, w_x, w_a, w_z, conv, d_rows, z_bias, w_out, w13, w2, c_t, wmod,
                         consts, head_hot, out):
    with ExitStack() as ctx:
        def sb(name, shape, dt, where=ctx):
            return where.enter_context(nc.sbuf_tensor(name, shape, dt))

        def sem(name):
            return ctx.enter_context(nc.semaphore(name))

        ps = ctx.enter_context(nc.psum_tensor("ps", [P, 8, BANK], F32))

        ht_hi = sb("ht_hi", [P, KT, B * L], F32R)
        ht_lo = sb("ht_lo", [P, KT, B * L], F32R)
        x_tok = sb("x_tok", [P, TT, D], F32)
        cst = sb("cst", [P, 5, P], F32)
        ident, triu, strict, ones, hadamard = (cst[:, i, :] for i in range(5))
        wo_sb = sb("wo_sb", [P, KT, D], F32)
        wz_raw = sb("wz_raw", [P, 2, KT, P], F32)
        wz_hi = sb("wz_hi", [P, 2, KT, P], F32R)
        wz_lo = sb("wz_lo", [P, 2, KT, P], F32R)
        zb_sb = sb("zb_sb", [P, 2], F32)
        gates = sb("gates", [P, B, 2, D], F32)
        shift = sb("shift", [P, 2, KT, B], F32)
        scale1 = sb("scale1", [P, 2, KT, B], F32)
        stats = sb("stats", [P, CH, 6], F32)
        meanvar = sb("meanvar", [P, CH, 2], F32)
        vareps = sb("vareps", [P, CH], F32)
        rstd = sb("rstd", [P, CH], F32)
        minus_half = sb("minus_half", [P, CH], F32)
        ident_bf = sb("ident_bf", [P, P], BF16)
        stage = sb("stage", [P, 2 * NM * D], F32)

        reg_a = ExitStack()
        wmod_sb = sb("wmod_sb", [P, KT, 6 * D], F32, reg_a)
        u_sb = sb("u_sb", [P, TT, D], F32, reg_a)
        xn = sb("xn", [P, 2, CH, D], F32, reg_a)
        wx_raw = sb("wx_raw", [P, 2, KT, P], F32, reg_a)
        wx_hi = sb("wx_hi", [P, 2, KT, P], F32R, reg_a)
        wx_lo = sb("wx_lo", [P, 2, KT, P], F32R, reg_a)
        h32 = sb("h32", [P, KT, L], F32, reg_a)
        reg_a.close()
        w13_hi = sb("w13_hi", [P, NM, 2, KT, P], F32R)
        w13_lo = sb("w13_lo", [P, NM, 2, KT, P], F32R)
        w2_hi = sb("w2_hi", [P, NM, D], F32R)
        w2_lo = sb("w2_lo", [P, NM, D], F32R)

        reg_b = ExitStack()
        c_sb = sb("c_sb", [P, KT, B], F32, reg_b)
        c_exp = sb("c_exp", [P, KT, B], F32, reg_b)
        c_silu = sb("c_silu", [P, KT, B], F32, reg_b)
        p_tok = sb("p_tok", [P, TT, NH], F32, reg_b)
        e_tok = sb("e_tok", [P, TT, NH], F32, reg_b)
        dec = sb("dec", [P, NV, B, NH], F32, reg_b)
        pT = sb("pT", [3 * NH, TT * P], BF16, reg_b)
        sel = sb("sel", [3 * NH, NH, P], BF16, reg_b)
        hot_sb = sb("hot_sb", [3 * NH, NH], F32, reg_b)
        conv_sb = sb("conv_sb", [P, NG * GT + 2, TAPS + 1], F32, reg_b)
        d_sb = sb("d_sb", [P, NH], F32, reg_b)
        wg_raw = sb("wg_raw", [P, GT, KT, P], F32, reg_b)
        wg_hi = sb("wg_hi", [P, GT, KT, P], F32R, reg_b)
        wg_lo = sb("wg_lo", [P, GT, KT, P], F32R, reg_b)
        cw_act = sb("cw_act", [P, GT, 2], F32, reg_b)
        cw_dve = sb("cw_dve", [P, GT, 3], F32, reg_b)
        p_slot = sb("p_slot", [P, TT, JH], F32, reg_b)
        acc = sb("acc", [P, 2, GT, L], F32, reg_b)
        decay = sb("decay", [P, JH, L], F32, reg_b)
        reg_c = ExitStack()
        c_rows = sb("c_rows", [P, KT, B, P], F32, reg_c)
        a_abs = sb("a_abs", [P, TT * NH], F32, reg_c)
        a_exp = sb("a_exp", [P, TT * NH], F32, reg_c)
        parts = sb("parts", [P, TT, 3, NH], BF16, reg_c)
        wa_raw = sb("wa_raw", [P, KT, NH], F32, reg_c)
        wa_hi = sb("wa_hi", [P, KT, NH], F32R, reg_c)
        wa_lo = sb("wa_lo", [P, KT, NH], F32R, reg_c)
        sp_a = sb("sp_a", [P, B, CH, NH], F32, reg_c)
        reg_c.close()
        mix = sb("mix", [P, JH, L], F32, reg_b)
        b_tok = sb("b_tok", [P, 2, 3 * P], F32, reg_b)
        yt_sb = sb("yt_sb", [2 * GC, L], F32, reg_b)
        xds = sb("xds", [P, 2, NV, GC], F32, reg_b)
        st_sb = sb("st_sb", [P, 2, 3, GC], F32, reg_b)
        xs = sb("xs", [P, 2, JH * (P + HD)], F32, reg_b)
        y_off = sb("y_off", [P, 3, GC], F32, reg_b)
        reg_b.close()
        hid_hi = sb("hid_hi", [P, NM, L], F32R)
        yv = sb("yv", [P, CH, D], F32)
        u2 = sb("u2", [P, CH, D], F32)
        sz = sb("sz", [P, KT, L], F32)
        gy = sb("gy", [P, KT, L], F32)
        hid_lo = sb("hid_lo", [P, NM, L], F32R)
        hid = sb("hid", [P, 2, L], F32)
        silu_sb = sb("silu_sb", [P, 2, L], F32)
        xn2 = sb("xn2", [P, CH, D], F32)
        h32b = sb("h32b", [P, KT, L], F32)
        h2_hi = sb("h2_hi", [P, KT, L], F32R)
        h2_lo = sb("h2_lo", [P, KT, L], F32R)
        ga_out = stage[:, 0:4 * D].rearrange("p (n c d) -> p n c d", n=2, c=2)
        gb_out = stage[:, 4 * D:6 * D].rearrange("p (n c d) -> p n c d", n=2, c=1)

        names = """
        ld_c ld_wmod ld_wmod2 ld_u0 ld_u1 ld_u2 ld_u3 ld_cst ld_wx ld_wa ld_conv ld_hot sel_done ld_d ld_wg ld_wz ld_zb ld_wo
        ld_w13 ld_w2 ld_res st_out
        c_exp_done c_one c_rec c_silu_done c_rows_done mod_mm mod_ev gate_mm gate_abs gate_sign gate_ev ident_done
        bnst bnag eps1 rs half_set xn_done lnT_mm h32_done hhi_done hlo_done wx_split wa_split wz_split
        xp_mm xtap xtaps xT_mm xtok_ev a_mm abs_done aexp_done aln_done sp_done ptok_mm dk_mm
        e_done dec_done p_copy part_step parts_done pT_mm pT_ev st_zero
        wraw_free w_split cwa cwd p_sl pool_waits dve_waits pe_waits proj tap0 taps bt bt_ev csb diff_done exp_done score mixed state st_copy masked
        xds_done xs_done xd_done inter intra yt_ev y_tok xs_zero yoff_done y_mid y_done
        w13_hi_done w13_split bfly w2_mm w2_hi_done w2_split
        yv_done z_mm yT_mm silu_z gated oproj res_mul x1_done bn2 ag2 eps2 rs2 xn2_done lnT2 h32b_done h2hi_done h2lo_done
        up_mm silu_done hid_done hhi2 hlo2 down_mm out_mul x2_done
        """.split()
        s = {n: sem(n) for n in names}

        block = ctx.enter_context(nc.Block())

        @block.sync
        def _(sp):
            def load(dst, src, name):
                sp.dma_start(dst, src).then_inc(s[name], 16)

            u_b = u.rearrange("(b c p) d -> b p c d", b=B, p=P)
            out_b = out.rearrange("(b c p) d -> b p c d", b=B, p=P)
            load(c_sb[:], c_t, "ld_c")
            load(u_sb[:, 0:CH, :], u_b[0], "ld_u0")
            load(cst[:], consts, "ld_cst")
            load(wmod_sb[:, :, 0:2 * D], wmod[:, :, 0:2 * D], "ld_wmod")
            load(wx_raw[:], w_x, "ld_wx")
            load(wa_raw[:], w_a, "ld_wa")
            load(conv_sb[:], conv, "ld_conv")
            for b in range(1, B):
                load(u_sb[:, b * CH:(b + 1) * CH, :], u_b[b], f"ld_u{b}")
            load(wg_raw[:], w_bc[0], "ld_wg")
            load(wmod_sb[:, :, 2 * D:], wmod[:, :, 2 * D:], "ld_wmod2")
            load(hot_sb[:], head_hot, "ld_hot")
            load(d_sb[:], d_rows, "ld_d")
            load(wz_raw[:], w_z, "ld_wz")
            load(zb_sb[:], z_bias, "ld_zb")
            load(wo_sb[:], w_out, "ld_wo")
            load(stage[:], w13, "ld_w13")
            with sp.Fori(1, NG) as g:
                sp.wait_ge(s["w_split"], g * (2 * GT))
                sp.dma_start(wg_raw[:], w_bc[bass.ds(g, 1)].rearrange("a p t k m -> p (a t) k m")).then_inc(s["ld_wg"], 16)
            sp.wait_ge(s["w13_split"], NM)
            load(stage[:, 0:NM * D], w2, "ld_w2")
            sp.wait_ge(s["xd_done"], NG * B)
            sp.wait_ge(s["proj"], NG * B * GT)
            for b in range(B):
                if b:
                    sp.wait_ge(s["x1_done"], 2 * b)
                load(u2[:], u_b[b], "ld_res")
            for b in range(B):
                sp.wait_ge(s["x2_done"], SLOTS + CH * (b + 1))
                sp.dma_start(out_b[b], x_tok[:, b * CH:(b + 1) * CH, :]).then_inc(s["st_out"], 16)
            sp.wait_ge(s["st_out"], 16 * B)

        @block.tensor
        def _(pe):
            mm = nc.tensor.matmul

            def split_mm(o, w_hi, w_lo, x_hi, x_lo, first, last):
                mm(o, w_hi, x_hi, start=first, stop=False)
                mm(o, w_hi, x_lo, start=False, stop=False)
                return mm(o, w_lo, x_hi, start=False, stop=last)

            def modulation(kinds, bank):
                pe.wait_ge(s["c_silu_done"], 1)
                for k, kind in enumerate(kinds):
                    for m in range(KT):
                        o = ps[:, bank, (2 * k + m) * B:(2 * k + m + 1) * B]
                        for kt in range(KT):
                            i = mm(o, wmod_sb[:, kt, kind * D + m * P:kind * D + (m + 1) * P], c_silu[:, kt, :],
                                   start=(kt == 0), stop=(kt == KT - 1))
                i.then_inc(s["mod_mm"], 1)

            def norm_transposes(b):
                pe.wait_ge(s["xn_done"], CH * (b + 1))
                if b:
                    pe.wait_ge(s["h32_done"], KT * b)
                for c in range(CH):
                    for kt in range(KT):
                        i = nc.tensor.transpose(ps[:, 2 + kt, c * P:(c + 1) * P],
                                                xn[:, b % 2, c, kt * P:(kt + 1) * P], ident)
                i.then_inc(s["lnT_mm"], 1)

            def gate_rows(b):
                if b < 2:
                    pe.wait_ge(s["h32_done"], KT * B)
                else:
                    pe.wait_ge(s["gate_ev"], b - 1)
                for k, kind in enumerate((2, 5)):
                    for kt in range(KT):
                        i = mm(ps[:, 2 + b % 2, k * D:(k + 1) * D], c_rows[:, kt, b, :],
                               wmod_sb[:, kt, kind * D:(kind + 1) * D], start=(kt == 0), stop=(kt == KT - 1))
                i.then_inc(s["gate_mm"], 1)

            def x_project(b):
                pe.wait_ge(s["hlo_done"], KT * (b + 1))
                for xt in range(2):
                    n = 2 * b + xt
                    if n >= 2:
                        pe.wait_ge(s["xtaps"], 3 * (n - 1))
                    for kt in range(KT):
                        i = split_mm(ps[:, xt, :], wx_hi[:, xt, kt, :], wx_lo[:, xt, kt, :],
                                     ht_hi[:, kt, b * L:(b + 1) * L], ht_lo[:, kt, b * L:(b + 1) * L],
                                     kt == 0, kt == KT - 1)
                    i.then_inc(s["xp_mm"], 1)

            def a_project(b):
                for c in range(CH):
                    t = b * CH + c
                    for kt in range(KT):
                        i = split_mm(ps[:, 6, t * NH:(t + 1) * NH],
                                     ht_hi[:, kt, t * P:(t + 1) * P], ht_lo[:, kt, t * P:(t + 1) * P],
                                     wa_hi[:, kt, :], wa_lo[:, kt, :], kt == 0, kt == KT - 1)
                if b == B - 1:
                    i.then_inc(s["a_mm"], 1)

            def x_transposes(b):
                for xt in range(2):
                    n = 2 * b + xt
                    pe.wait_ge(s["xtaps"], 3 * (n + 1))
                    if n >= 2:
                        pe.wait_ge(s["xtok_ev"], n - 1)
                    for c in range(CH):
                        i = nc.tensor.transpose(ps[:, 4 + xt, c * P:(c + 1) * P],
                                                acc[:, n // GT, n % GT, c * P:(c + 1) * P], ident)
                    i.then_inc(s["xT_mm"], 1)

            pe.wait_ge(s["ld_cst"], 16)
            norm_transposes(0)
            pe.wait_ge(s["ld_wmod"], 16)
            modulation((0, 1), 0)
            pe.wait_ge(s["mod_ev"], 2)
            pe.wait_ge(s["wx_split"], 2)
            pe.wait_ge(s["wa_split"], 2)
            for b in range(B):
                if b + 1 < B:
                    norm_transposes(b + 1)
                x_project(b)
                a_project(b)
                if b:
                    x_transposes(b - 1)
            pe.wait_ge(s["ld_wmod2"], 16)
            modulation((3, 4), 7)
            pe.wait_ge(s["c_rows_done"], KT * B)
            gate_rows(0)
            gate_rows(1)
            x_transposes(B - 1)

            pe.wait_ge(s["sp_done"], 1)
            pe.wait_ge(s["mod_ev"], 4)
            mm(ps[:, 7, :], triu, sp_a[:].rearrange("p b c h -> p (b c h)"), start=True,
               stop=True).then_inc(s["ptok_mm"], 1)
            pe.wait_ge(s["xtok_ev"], 2 * B)
            for c in range(CH - 1):
                for t in range(CH - 1 - c):
                    v = V0[c] + t
                    o = ps[:, 4 + v // 3, (v % 3) * B * NH:(v % 3 + 1) * B * NH]
                    i = mm(o, strict, sp_a[:, :, c, :], start=True, stop=(t == 0))
                    for k in range(t):
                        i = mm(o, ones, sp_a[:, :, c + 1 + k, :], start=False, stop=(k == t - 1))
            i.then_inc(s["dk_mm"], 1)
            def proj(g, b, t):
                n = (g * B + b) * GT + t
                if isinstance(g, int) and g == 0 and b == 0 and t < 2:
                    pass
                else:
                    pe.wait_ge(s["taps"], (n - 1) * 3)
                if b == 0:
                    pe.wait_ge(s["w_split"], (g * GT + t) * 2 + 2)
                for kt in range(KT):
                    i = split_mm(ps[:, t % 2, :], wg_hi[:, t, kt, :], wg_lo[:, t, kt, :],
                                 ht_hi[:, kt, b * L:(b + 1) * L], ht_lo[:, kt, b * L:(b + 1) * L],
                                 kt == 0, kt == KT - 1)
                i.then_inc(s["proj"], 1)

            def b_transposes(q, b, p, first):
                pe.wait_ge(s["taps"], 12 * q + 3 * (p + 1))
                if not first or p:
                    pe.wait_ge(s["bt_ev"], 2 * q + p)
                for c in range(CH - 1):
                    i = nc.tensor.transpose(ps[:, 6, c * P:(c + 1) * P],
                                            acc[:, b % 2, p, c * P:(c + 1) * P], ident)
                i.then_inc(s["bt"], 1)

            def running_sums(g, q, b, j, first):
                if not first or j >= 2:
                    pe.wait_ge(s["diff_done"], 4 * q + j - 1)
                mm(ps[:, 4 + j % 2, :], sel[:, bass.ds(g * JH + j, 1), :].rearrange("p a m -> p (a m)"),
                   pT[:, b * L:(b + 1) * L], start=True, stop=True).then_inc(s["csb"], 1)

            def scores(q, b, p, first):
                pe.wait_ge(s["taps"], 12 * q + 3 * (3 + p))
                if not first or p:
                    pe.wait_ge(s["mixed"], 4 * q + 2 * p)
                for c in range(CH):
                    for a in range(2):
                        i = mm(ps[:, 2 + a, c * P:(c + 1) * P],
                               acc[NS * a:NS * (a + 1), b % 2, p, c * P:(c + 1) * P],
                               acc[NS * a:NS * (a + 1), b % 2, 2 + p, c * P:(c + 1) * P],
                               start=True, stop=True)
                        if c == CH - 1:
                            i.then_inc(s["score"], 1)

            def states(q, b):
                pe.wait_ge(s["bt_ev"], 2 * q + 2)
                pe.wait_ge(s["xds_done"], 3 * q + 3)
                for p in range(2):
                    for c in range(CH - 1):
                        n = CH - 1 - c
                        o = ps[:, 6, 3 * P + p * 48 + c * 16:3 * P + (p + 1) * 48]
                        i = mm(o, b_tok[:, p, c * P:(c + 1) * P],
                               xds[:, b % 2, V0[c]:V0[c] + n, 16 * p:16 * (p + 1)],
                               start=(c == 0), stop=(c == CH - 2))
                i.then_inc(s["state"], 1)

            def inter(q, b, first):
                pe.wait_ge(s["st_copy"], 2 * q + 2)
                if not first:
                    pe.wait_ge(s["yoff_done"], q)
                    pe.wait_ge(s["y_mid"], q)
                for c in range(1, CH):
                    for p in range(2):
                        i = mm(ps[GC:2 * GC, 7, c * P:(c + 1) * P], st_sb[:, p, c - 1, :],
                               acc[:, b % 2, 2 + p, c * P:(c + 1) * P], start=(p == 0), stop=(p == 1))
                i.then_inc(s["inter"], 1)

            def intra(q, b):
                pe.wait_ge(s["xs_done"], q + 1)
                pe.wait_ge(s["mixed"], 4 * q + 4)
                for c in range(CH):
                    for j in range(JH):
                        k = j * P + c * GC
                        i = mm(ps[0:GC, 7, c * P:(c + 1) * P], xs[:, b % 2, k:k + GC],
                               mix[:, j, c * P:(c + 1) * P], start=(j == 0), stop=(j == JH - 1))
                i.then_inc(s["intra"], 1)

            def y_transposes(q):
                pe.wait_ge(s["yt_ev"], 2 * q + 2)
                pe.sem_inc(s["pe_waits"], 1)
                for c in range(CH):
                    rows = 2 * GC if c else GC
                    i = nc.tensor.transpose(ps[:, 7, c * 2 * GC:c * 2 * GC + rows],
                                            yt_sb[0:rows, c * P:(c + 1) * P], cst[0:rows, 0, 0:rows])
                i.then_inc(s["y_tok"], 1)

            def w2_transform(n):
                if n < 2:
                    pe.wait_ge(s["taps"], NG * B * GT * 3)
                else:
                    pe.wait_ge(s["mixed"], NG * B * JH)
                mm(ps[:, n, :], hadamard, stage[:, NM * D + n * BANK:NM * D + (n + 1) * BANK], start=True,
                   stop=True).then_inc(s["w2_mm"], 1)

            def z_project(b, zt):
                if not isinstance(b, int):
                    pe.wait_ge(s["hid_done"], NM * (b - 1))
                elif b == 0:
                    pe.wait_ge(s["w2_split"], zt + 1)
                else:
                    pe.wait_ge(s["silu_z"], zt + 1)
                for kt in range(KT):
                    x0 = ht_hi[:, kt, bass.ds(b * L, L)]
                    x1 = ht_lo[:, kt, bass.ds(b * L, L)]
                    i = split_mm(ps[:, zt, :], wz_hi[:, zt, kt, :], wz_lo[:, zt, kt, :], x0, x1, kt == 0, kt == KT - 1)
                i.then_inc(s["z_mm"], 1)

            def step(g, b, gq=None, gr=None):
                bq, br = (b - 1) % B, (b - 2) % B
                q = gq * B + bq if gq is not None else None
                r = gr * B + br if gr is not None else None
                first = r is None
                project = g is not None
                if not project:
                    pe.wait_ge(s["bfly"], 6)
                    pe.wait_ge(s["wz_split"], 2)
                if q is not None:
                    b_transposes(q, bq, 0, first)
                    running_sums(gq, q, bq, 0, first)
                    running_sums(gq, q, bq, 1, first)
                if project:
                    proj(g, b, 0)
                else:
                    w2_transform(0)
                if r is not None:
                    intra(r, br)
                if q is not None:
                    running_sums(gq, q, bq, 2, first)
                    running_sums(gq, q, bq, 3, first)
                    scores(q, bq, 0, first)
                    b_transposes(q, bq, 1, first)
                if project:
                    proj(g, b, 1)
                else:
                    w2_transform(1)
                if r is not None:
                    y_transposes(r)
                if q is not None:
                    scores(q, bq, 1, first)
                if project:
                    proj(g, b, 2)
                else:
                    z_project(0, 0)
                if q is not None:
                    states(q, bq)
                if project:
                    proj(g, b, 3)
                else:
                    z_project(0, 1)
                if q is not None:
                    inter(q, bq, first)

            pe.wait_ge(s["xtaps"], 3 * 2 * B)
            proj(0, 0, 0)
            proj(0, 0, 1)
            pe.wait_ge(s["parts_done"], 1)
            pe.wait_ge(s["e_done"], 1)
            part_ps = ps[:, 6:8, :].rearrange("p k n -> p (k n)").bitcast(BF16)
            for t in range(TT):
                i = nc.tensor.transpose(part_ps[0:3 * NH, t * P:(t + 1) * P],
                                        parts[:, t, :, :].rearrange("p k h -> p (k h)"), ident_bf[:])
            i.then_inc(s["pT_mm"], 1)
            gate_rows(2)
            gate_rows(3)
            proj(0, 0, 2)
            proj(0, 0, 3)
            pe.wait_ge(s["pT_ev"], 2)
            pe.wait_ge(s["gate_ev"], B)
            pe.wait_ge(s["dec_done"], 1)
            pe.wait_ge(s["p_copy"], 1)
            pe.wait_ge(s["st_zero"], 1)
            pe.wait_ge(s["xs_zero"], 1)
            pe.wait_ge(s["sel_done"], 1)
            for b in range(1, B):
                step(0, b, gq=0, gr=(None if b == 1 else 0))
            with pe.Fori(1, NG) as g:
                for b in range(B):
                    step(g, b, gq=(g - 1 if b == 0 else g), gr=(g - 1 if b < 2 else g))
            step(None, 0, gq=NG - 1, gr=NG - 1)
            intra(NG * B - 1, B - 1)

            def yT_transposes(b, bank):
                if isinstance(b, int):
                    src = x_tok[:, b * CH:(b + 1) * CH, :]
                    pe.wait_ge(s["y_done"], (NG - 1) * B + b + 1)
                else:
                    src = yv
                    pe.wait_ge(s["yv_done"], b - 1)
                    pe.wait_ge(s["x1_done"], 2 * b)
                for kt in range(KT):
                    for c in range(CH):
                        i = nc.tensor.transpose(ps[:, bank + kt, c * P:(c + 1) * P], src[:, c, kt * P:(kt + 1) * P], ident)
                    i.then_inc(s["yT_mm"], 1)

            def out_project(b, bank):
                pe.wait_ge(s["gated"], KT * (b + 1))
                for c in range(CH):
                    for kt in range(KT):
                        i = mm(ps[:, bank + c // 2, (c % 2) * D:(c % 2 + 1) * D], gy[:, kt, c * P:(c + 1) * P],
                               wo_sb[:, kt, :], start=(kt == 0), stop=(kt == KT - 1))
                    if c % 2:
                        i.then_inc(s["oproj"], 1)

            def norm2_transposes(b):
                pe.wait_ge(s["xn2_done"], CH * (b + 1))
                for kt in range(KT):
                    for c in range(CH):
                        i = nc.tensor.transpose(ps[:, 6 + kt, c * P:(c + 1) * P], xn2[:, c, kt * P:(kt + 1) * P], ident)
                    i.then_inc(s["lnT2"], 1)

            def up(b, fronts):
                pe.wait_ge(s["h2lo_done"], KT * (b + 1))
                pe.wait_ge(s["silu_z"], KT * fronts)
                pe.wait_ge(s["x1_done"], 2 * fronts)
                for m in range(NM):
                    if m >= 2:
                        pe.wait_ge(s["hid_done"], b * NM + m - 1)
                    for half in range(2):
                        for kt in range(KT):
                            i = split_mm(ps[:, 2 * half + m % 2, :], w13_hi[:, m, half, kt, :],
                                         w13_lo[:, m, half, kt, :], h2_hi[:, kt, :], h2_lo[:, kt, :],
                                         kt == 0, kt == KT - 1)
                    i.then_inc(s["up_mm"], 1)

            def down(b, c):
                if c == 0:
                    pe.wait_ge(s["hlo2"], SLOTS + NM * (b + 1))
                pe.wait_ge(s["out_mul"], b * CH + c + 1)
                for m in range(NM):
                    i = split_mm(ps[:, 4 + c % 2, 0:D], hid_hi[:, m, c * P:(c + 1) * P], hid_lo[:, m, c * P:(c + 1) * P],
                                 w2_hi[:, m, :], w2_lo[:, m, :], m == 0, m == NM - 1)
                i.then_inc(s["down_mm"], 1)

            def ffn_step(b, normed, ahead):
                up(b, b + 2 if normed else B)
                if normed:
                    norm2_transposes(b + 1)
                if ahead:
                    z_project(b + 2, 0)
                    z_project(b + 2, 1)
                down(b, 0)
                if ahead:
                    yT_transposes(b + 2, 2)
                down(b, 1)
                if ahead:
                    out_project(b + 2, 2)
                down(b, 2)
                down(b, 3)

            pe.wait_ge(s["diff_done"], NG * B * JH)
            yT_transposes(0, 4)
            w2_transform(2)
            w2_transform(3)
            y_transposes(NG * B - 1)
            pe.wait_ge(s["ld_wo"], 16)
            out_project(0, 4)
            z_project(1, 0)
            z_project(1, 1)
            pe.wait_ge(s["w2_split"], 4)
            yT_transposes(1, 2)
            pe.wait_ge(s["y_done"], NG * B)
            norm2_transposes(0)
            out_project(1, 2)
            with pe.Fori(0, B - 2) as b:
                ffn_step(b, True, True)
            ffn_step(B - 2, True, False)
            ffn_step(B - 1, False, False)

        @block.scalar
        def _(act):
            af = nc.scalar.activation

            act.wait_ge(s["ld_c"], 16)
            af(c_exp[:], c_sb[:], ACT.Exp, scale=-1.0).then_inc(s["c_exp_done"], 1)

            def h_parts(b):
                act.wait_ge(s["lnT_mm"], b + 1)
                for kt in range(KT):
                    n = KT * b + kt
                    if b:
                        act.wait_ge(s["hlo_done"], n - 1)
                    af(h32[:, kt, :], ps[:, 2 + kt, :], ACT.Identity, bias=shift[:, 0, kt, b:b + 1],
                       scale=scale1[:, 0, kt, b:b + 1]).then_inc(s["h32_done"], 1)
                for kt in range(KT):
                    act.wait_ge(s["h32_done"], KT * b + kt + 1)
                    nc.scalar.copy(ht_hi[:, kt, b * L:(b + 1) * L], h32[:, kt, :]).then_inc(s["hhi_done"], 1)

            def x_tap(b):
                for xt in range(2):
                    n = 2 * b + xt
                    act.wait_ge(s["xp_mm"], n + 1)
                    w = conv_sb[:, NG * GT + xt, :]
                    af(acc[:, n // GT, n % GT, :], ps[:, xt, :], ACT.Identity, bias=w[:, TAPS:TAPS + 1],
                       scale=w[:, TAPS - 1:TAPS]).then_inc(s["xtap"], 1)

            def x_evacuate(b):
                for xt in range(2):
                    n = 2 * b + xt
                    act.wait_ge(s["xT_mm"], n + 1)
                    nc.scalar.copy(x_tok[:, b * CH:(b + 1) * CH, xt * P:(xt + 1) * P],
                                   ps[:, 4 + xt, :].rearrange("p (c m) -> p c m", c=CH)).then_inc(s["xtok_ev"], 1)

            act.wait_ge(s["mod_ev"], 2)
            act.wait_ge(s["ld_conv"], 16)
            h_parts(0)
            for b in range(B):
                if b + 1 < B:
                    h_parts(b + 1)
                x_tap(b)
                if b:
                    x_evacuate(b - 1)

            def gate_size(b):
                act.wait_ge(s["gate_mm"], b + 1)
                af(gates[:, b].rearrange("p k d -> p (k d)"), ps[:, 2 + b % 2, :], ACT.Abs).then_inc(s["gate_abs"], 1)

            act.wait_ge(s["a_mm"], 1)
            af(a_abs[:], ps[:, 6, :], ACT.Abs).then_inc(s["abs_done"], 1)
            act.wait_ge(s["abs_done"], 1)
            af(a_exp[:], a_abs[:], ACT.Exp, scale=-1.0).then_inc(s["aexp_done"], 1)
            act.wait_ge(s["aexp_done"], 1)
            af(a_exp[:], a_exp[:], ACT.Ln, bias=1.0).then_inc(s["aln_done"], 1)
            x_evacuate(B - 1)
            act.wait_ge(s["p_copy"], 1)
            af(e_tok[:].rearrange("p t h -> p (t h)"), ps[:, 7, :], ACT.Exp, scale=-1.0).then_inc(s["e_done"], 1)
            act.wait_ge(s["dk_mm"], 1)
            for k in range(2):
                i = af(dec[:, 3 * k:3 * k + 3, :, :].rearrange("p v b h -> p (v b h)"), ps[:, 4 + k, 0:3 * B * NH],
                       ACT.Exp, scale=-1.0)
            i.then_inc(s["dec_done"], 1)
            gate_size(0)
            gate_size(1)
            act.wait_ge(s["pT_mm"], 1)
            for k in range(2):
                nc.scalar.copy(pT[:, k * 1024:(k + 1) * 1024],
                               ps[0:3 * NH, 6 + k, :].bitcast(BF16)).then_inc(s["pT_ev"], 1)

            def last_tap(g, b, t):
                n = (g * B + b) * GT + t
                act.wait_ge(s["proj"], n + 1)
                af(acc[:, b % 2, t, :], ps[:, t % 2, :], ACT.Identity, bias=cw_act[:, t, 1:2],
                   scale=cw_act[:, t, 0:1]).then_inc(s["tap0"], 1)

            def b_evacuate(q, p):
                act.wait_ge(s["bt"], 2 * q + p + 1)
                nc.scalar.copy(b_tok[:, p, :], ps[:, 6, 0:3 * P]).then_inc(s["bt_ev"], 1)

            def decays(q, b, j, first):
                act.wait_ge(s["csb"], 4 * q + j + 1)
                if not first:
                    act.wait_ge(s["mixed"], 4 * q + j - 3)
                for c in range(CH):
                    i = af(decay[:, j, c * P:(c + 1) * P], ps[:, 4 + j % 2, c * P:(c + 1) * P], ACT.Relu,
                           bias=p_slot[:, b * CH + c, j:j + 1])
                i.then_inc(s["diff_done"], 1)
                act.wait_ge(s["diff_done"], 4 * q + j + 1)
                af(decay[:, j, :], decay[:, j, :], ACT.Exp, scale=-1.0).then_inc(s["exp_done"], 1)

            def inter_evacuate(r, start):
                act.wait_ge(s["inter"], r + 1)
                if not start:
                    act.wait_ge(s["y_tok"], r)
                nc.scalar.copy(yt_sb[GC:2 * GC, P:], ps[GC:2 * GC, 7, P:]).then_inc(s["yt_ev"], 1)

            def intra_evacuate(r):
                act.wait_ge(s["intra"], r + 1)
                nc.scalar.copy(yt_sb[0:GC, :], ps[0:GC, 7, :]).then_inc(s["yt_ev"], 1)

            def w2_upper(n):
                act.wait_ge(s["w2_mm"], n + 1)
                nc.scalar.copy(w2_hi[:, 2 * n:2 * n + 2, :].rearrange("p m d -> p (m d)"),
                               ps[:, n, :]).then_inc(s["w2_hi_done"], 1)

            def step(g, b, attend=True, project=True, gq=None, gr=None, first=False):
                bq = (b - 1) % B
                q = gq * B + bq if attend else None
                first_r = isinstance(gr, int) and gr == 0 and b == 2
                if project and b == 0:
                    if attend:
                        act.wait_ge(s["tap0"], g * (GT * B))
                    nc.scalar.copy(cw_act[:], conv_sb[:, bass.ds(g * GT, GT), TAPS - 1:TAPS + 1]).then_inc(s["cwa"], 1)
                if project and b == 1:
                    act.wait_ge(s["exp_done"], g * 4 * B) if not (isinstance(g, int) and g == 0) else None
                    nc.scalar.mul(p_slot[:], p_tok[:, :, bass.ds(g * JH, JH)], -1.0).then_inc(s["p_sl"], 1)
                    act.wait_ge(s["p_sl"], g + 1)
                if attend:
                    b_evacuate(q, 0)
                    decays(q, bq, 0, first)
                if gr is not None:
                    inter_evacuate(gr * B + (b - 2) % B, first_r)
                if project:
                    if b == 0:
                        act.wait_ge(s["cwa"], g + 1)
                    last_tap(g, b, 0)
                else:
                    w2_upper(0)
                if attend:
                    decays(q, bq, 1, first)
                if gr is not None:
                    intra_evacuate(gr * B + (b - 2) % B)
                if attend:
                    decays(q, bq, 2, first)
                    b_evacuate(q, 1)
                if project:
                    last_tap(g, b, 1)
                else:
                    w2_upper(1)
                if attend:
                    decays(q, bq, 3, first)
                if project:
                    last_tap(g, b, 2)
                    last_tap(g, b, 3)

            act.wait_ge(s["xT_mm"], 2 * B)
            nc.scalar.copy(cw_act[:], conv_sb[:, 0:GT, TAPS - 1:TAPS + 1]).then_inc(s["cwa"], 1)
            act.wait_ge(s["cwa"], 1)
            last_tap(0, 0, 0)
            last_tap(0, 0, 1)
            gate_size(2)
            gate_size(3)
            last_tap(0, 0, 2)
            last_tap(0, 0, 3)
            for b in range(1, B):
                step(0, b, gq=0, gr=(None if b == 1 else 0), first=(b == 1))
            with act.Fori(1, NG) as g:
                for b in range(B):
                    step(g, b, gq=(g - 1 if b == 0 else g), gr=(g - 1 if b < 2 else g))
            step(None, 0, gq=NG - 1, gr=NG - 1, project=False)

            def silu_gate(b):
                for zt in range(2):
                    act.wait_ge(s["z_mm"], 2 * b + zt + 1)
                    if not (isinstance(b, int) and b == 0):
                        act.wait_ge(s["gated"], KT * (b - 1) + zt + 1)
                    af(sz[:, zt, :], ps[:, zt, :], ACT.Silu, bias=zb_sb[:, zt:zt + 1]).then_inc(s["silu_z"], 1)

            def h2_parts(b):
                for kt in range(KT):
                    act.wait_ge(s["lnT2"], KT * b + kt + 1)
                    af(h32b[:, kt, :], ps[:, 6 + kt, :], ACT.Identity, bias=shift[:, 1, kt, bass.ds(b, 1)],
                       scale=scale1[:, 1, kt, bass.ds(b, 1)]).then_inc(s["h32b_done"], 1)
                for kt in range(KT):
                    act.wait_ge(s["h32b_done"], KT * b + kt + 1)
                    nc.scalar.copy(h2_hi[:, kt, :], h32b[:, kt, :]).then_inc(s["h2hi_done"], 1)

            def hidden(b):
                for m in range(NM):
                    n = b * NM + m
                    act.wait_ge(s["up_mm"], n + 1)
                    af(silu_sb[:, m % 2, :], ps[:, m % 2, :], ACT.Silu).then_inc(s["silu_done"], 1)
                    act.wait_ge(s["hid_done"], n + 1)
                    nc.scalar.copy(hid_hi[:, m, :], hid[:, m % 2, :]).then_inc(s["hhi2"], 1)

            act.wait_ge(s["ld_zb"], 16)
            inter_evacuate(NG * B - 1, False)
            silu_gate(0)
            intra_evacuate(NG * B - 1)
            w2_upper(2)
            w2_upper(3)
            silu_gate(1)
            h2_parts(0)
            with act.Fori(0, B - 2) as b:
                hidden(b)
                h2_parts(b + 1)
                silu_gate(b + 2)
            hidden(B - 2)
            h2_parts(B - 1)
            hidden(B - 1)

        @block.vector
        def _(dve):
            ts = nc.vector.tensor_scalar
            tt = nc.vector.tensor_tensor
            stt = nc.vector.scalar_tensor_tensor

            dve.wait_ge(s["c_exp_done"], 1)
            ts(c_exp[:], c_exp[:], 1.0, None, ALU.add).then_inc(s["c_one"], 1)
            dve.wait_ge(s["c_one"], 1)
            nc.vector.reciprocal(c_exp[:], c_exp[:]).then_inc(s["c_rec"], 1)
            dve.wait_ge(s["c_rec"], 1)
            tt(c_silu[:], c_sb[:], c_exp[:], ALU.mult).then_inc(s["c_silu_done"], 1)
            dve.wait_ge(s["c_silu_done"], 1)
            def normalise(src, dst, n, names):
                st, ag, ep, rs, done = names
                for c in range(CH):
                    nc.vector.bn_stats(stats[:, c, :], src[:, c, :]).then_inc(s[st], 1)
                for c in range(CH):
                    dve.wait_ge(s[st], n * CH + c + 1)
                    dve.sem_inc(s["dve_waits"], 1)
                    nc.vector.bn_aggr(meanvar[:, c, :], stats[:, c, :]).then_inc(s[ag], 1)
                dve.wait_ge(s[ag], n * CH + CH)
                ts(vareps[:], meanvar[:, :, 1], EPS, None, ALU.add).then_inc(s[ep], 1)
                dve.wait_ge(s[rs], n + 1)
                for c in range(CH):
                    ts(dst[:, c, :], src[:, c, :], meanvar[:, c, 0:1], rstd[:, c:c + 1], ALU.subtract,
                       ALU.mult).then_inc(s[done], 1)

            def norm1(b):
                dve.wait_ge(s[f"ld_u{b}"], 16)
                if b >= 2:
                    dve.wait_ge(s["lnT_mm"], b - 1)
                normalise(u_sb[:, b * CH:(b + 1) * CH, :], xn[:, b % 2], b, ("bnst", "bnag", "eps1", "rs", "xn_done"))

            def taps(a, bank, w, name, n, between=()):
                for k in range(TAPS - 1):
                    d = k + 1
                    if k:
                        dve.wait_ge(s[name], n + k)
                    stt(a[:, d:], ps[:, bank, 0:L - d], w[:, TAPS - 1 - d:TAPS - d], a[:, d:], ALU.mult,
                        ALU.add).then_inc(s[name], 1)
                    if k < len(between):
                        between[k]()

            def x_taps(b):
                for xt in range(2):
                    n = 2 * b + xt
                    dve.wait_ge(s["xtap"], n + 1)
                    taps(acc[:, n // GT, n % GT, :], xt, conv_sb[:, NG * GT + xt, :], "xtaps", 3 * n)

            def modulation(n):
                dve.wait_ge(s["mod_mm"], n + 1)
                mod = ps[:, 7 * n, 0:2 * KT * B].rearrange("p (k m b) -> p k m b", k=2, m=KT)
                nc.vector.tensor_copy(shift[:, n], mod[:, 0]).then_inc(s["mod_ev"], 1)
                ts(scale1[:, n], mod[:, 1], 1.0, None, ALU.add).then_inc(s["mod_ev"], 1)

            def gate_rows(b):
                gp = ps[:, 2 + b % 2, :]
                gt = gates[:, b].rearrange("p k d -> p (k d)")
                sign = xn[:, b % 2, 0:2, :].rearrange("p c d -> p (c d)")
                dve.wait_ge(s["gate_abs"], b + 1)
                if b < 2:
                    dve.wait_ge(s["lnT_mm"], B)
                else:
                    dve.wait_ge(s["gate_ev"], b - 1)
                ts(sign, gp, 0.0, 2.0, ALU.is_ge, ALU.mult).then_inc(s["gate_sign"], 1)
                ts(gt, gt, 0.25, None, ALU.max).then_inc(s["gate_sign"], 1)
                dve.wait_ge(s["gate_sign"], 2 * b + 2)
                stt(gt, sign, -1.0, gt, ALU.add, ALU.mult).then_inc(s["gate_ev"], 1)

            norm1(0)
            dve.wait_ge(s["ld_wx"], 16)
            nc.vector.tensor_copy(wx_hi[:], wx_raw[:]).then_inc(s["wx_split"], 1)
            dve.wait_ge(s["wx_split"], 1)
            tt(wx_lo[:], wx_raw[:], wx_hi[:].bitcast(F32), ALU.subtract).then_inc(s["wx_split"], 1)
            modulation(0)
            dve.wait_ge(s["ld_wa"], 16)
            nc.vector.tensor_copy(wa_hi[:], wa_raw[:]).then_inc(s["wa_split"], 1)
            dve.wait_ge(s["wa_split"], 1)
            tt(wa_lo[:], wa_raw[:], wa_hi[:].bitcast(F32), ALU.subtract).then_inc(s["wa_split"], 1)
            norm1(1)
            for kt in range(KT):
                for b in range(B):
                    nc.vector.tensor_copy(c_rows[:, kt, b, :],
                                          c_silu[:, kt, b:b + 1].to_broadcast([P, P])).then_inc(s["c_rows_done"], 1)
            nc.vector.memset(st_sb[:], 0.0).then_inc(s["st_zero"], 1)
            nc.vector.memset(xs[:], 0.0).then_inc(s["xs_zero"], 1)
            nc.vector.tensor_copy(ident_bf[:], ident).then_inc(s["ident_done"], 1)
            for b in range(B):
                if b + 2 < B:
                    norm1(b + 2)
                dve.wait_ge(s["ld_conv"], 16)
                x_taps(b)

            dve.wait_ge(s["aln_done"], 1)
            stt(sp_a[:].rearrange("p b c h -> p (b c h)"), ps[:, 6, :], 0.0, a_exp[:], ALU.max,
                ALU.add).then_inc(s["sp_done"], 1)
            modulation(1)
            dve.wait_ge(s["ptok_mm"], 1)
            nc.vector.tensor_copy(p_tok[:].rearrange("p t h -> p (t h)"), ps[:, 7, :]).then_inc(s["p_copy"], 1)
            dve.wait_ge(s["p_copy"], 1)
            rest = a_abs[:].rearrange("p (t h) -> p t h", h=NH)
            nc.vector.tensor_copy(parts[:, :, 0, :], p_tok[:]).then_inc(s["part_step"], 1)
            dve.wait_ge(s["part_step"], 1)
            tt(rest, p_tok[:], parts[:, :, 0, :], ALU.subtract).then_inc(s["part_step"], 1)
            dve.wait_ge(s["part_step"], 2)
            nc.vector.tensor_copy(parts[:, :, 1, :], rest).then_inc(s["part_step"], 1)
            dve.wait_ge(s["part_step"], 3)
            tt(parts[:, :, 2, :], rest, parts[:, :, 1, :], ALU.subtract).then_inc(s["parts_done"], 1)
            gate_rows(0)
            gate_rows(1)

            def mix_head(q, j, first):
                dve.wait_ge(s["score"], 4 * q + j + 1)
                dve.wait_ge(s["masked"], 4 * q + j + 1)
                if not first:
                    dve.wait_ge(s["intra"], q)
                tt(mix[:, j, :], ps[:, 2 + j % 2, :], decay[:, j, :], ALU.mult).then_inc(s["mixed"], 1)

            def conv_tile(g, b, t, between=()):
                n = (g * B + b) * GT + t
                dve.wait_ge(s["tap0"], n + 1)
                taps(acc[:, b % 2, t, :], t % 2, cw_dve[:, t, :], "taps", 3 * n, between)

            def copy_states(q, first):
                dve.wait_ge(s["state"], q + 1)
                for a in range(2):
                    src = ps[NS * a:NS * (a + 1), 6, 3 * P:3 * P + 96].rearrange("n (p t w) -> n p t w", p=2, t=3)
                    for p in range(2):
                        k = 2 * HD * p + HD * a
                        i = nc.vector.tensor_copy(st_sb[NS * a:NS * (a + 1), p, :, k:k + HD],
                                                  src[:, p, :, HD * a:HD * (a + 1)])
                    i.then_inc(s["st_copy"], 1)

            def y_combine(gq, q, b):
                x = x_tok[:, b * CH:(b + 1) * CH, bass.ds(gq * GC, GC)]
                x_later = x_tok[:, b * CH + 1:(b + 1) * CH, bass.ds(gq * GC, GC)]
                y = ps[:, 7, 0:2 * P].rearrange("p (c k w) -> p c k w", c=CH, k=2)

                def from_earlier():
                    dve.wait_ge(s["y_tok"], q + 1)
                    e = e_tok[:, b * CH + 1:(b + 1) * CH, bass.ds(gq * JH, JH)]
                    tt(y_off[:].rearrange("p c (j e) -> p c j e", j=JH),
                       y[:, 1:, 1].rearrange("p c (j e) -> p c j e", j=JH),
                       e.unsqueeze(3).to_broadcast([P, 3, JH, HD]), ALU.mult).then_inc(s["yoff_done"], 1)

                def inside():
                    dve.wait_ge(s["xd_done"], q + 1)
                    tt(x, y[:, :, 0], x, ALU.add).then_inc(s["y_mid"], 1)

                def total():
                    dve.wait_ge(s["yoff_done"], q + 1)
                    dve.wait_ge(s["y_mid"], q + 1)
                    tt(x_later, x_later, y_off[:], ALU.add).then_inc(s["y_done"], 1)

                return from_earlier, inside, total

            def w2_lower(n):
                dve.wait_ge(s["w2_hi_done"], n + 1)
                w = w2_lo[:, 2 * n:2 * n + 2, :].rearrange("p m d -> p (m d)")
                h = w2_hi[:, 2 * n:2 * n + 2, :].rearrange("p m d -> p (m d)")
                tt(w, ps[:, n, :], h.bitcast(F32), ALU.subtract).then_inc(s["w2_split"], 1)

            def step(g, b, attend=True, project=True, gq=None, gr=None, first=False):
                bq = (b - 1) % B
                q = gq * B + bq if attend else None
                if project and b == 0:
                    if attend:
                        dve.wait_ge(s["taps"], g * (3 * GT * B))
                    nc.vector.tensor_copy(cw_dve[:], conv_sb[:, bass.ds(g * GT, GT), 0:3]).then_inc(s["cwd"], 1)
                if project:
                    if b == 0:
                        dve.wait_ge(s["cwd"], g + 1)
                    conv_tile(g, b, 0)
                if attend:
                    mix_head(q, 0, first)
                    mix_head(q, 1, first)
                y_steps = y_combine(gr, gr * B + (b - 2) % B, (b - 2) % B) if gr is not None else ()
                if project:
                    conv_tile(g, b, 1, y_steps)
                else:
                    w2_lower(0)
                    for y_step in y_steps:
                        y_step()
                    w2_lower(1)
                if attend:
                    mix_head(q, 2, first)
                    mix_head(q, 3, first)
                    copy_states(q, first)
                if project:
                    conv_tile(g, b, 2)
                    conv_tile(g, b, 3)

            nc.vector.tensor_copy(cw_dve[:], conv_sb[:, 0:GT, 0:3]).then_inc(s["cwd"], 1)
            dve.wait_ge(s["cwd"], 1)
            conv_tile(0, 0, 0)
            conv_tile(0, 0, 1)
            gate_rows(2)
            gate_rows(3)
            conv_tile(0, 0, 2)
            conv_tile(0, 0, 3)
            for b in range(1, B):
                step(0, b, gq=0, gr=(None if b == 1 else 0), first=(b == 1))
            with dve.Fori(1, NG) as g:
                for b in range(B):
                    step(g, b, gq=(g - 1 if b == 0 else g), gr=(g - 1 if b < 2 else g))
            step(None, 0, gq=NG - 1, gr=NG - 1, project=False)

            def gate(b):
                for kt in range(KT):
                    dve.wait_ge(s["yT_mm"], KT * b + kt + 1)
                    dve.wait_ge(s["silu_z"], KT * b + kt + 1)
                    if not (isinstance(b, int) and b == 0):
                        dve.wait_ge(s["oproj"], 2 * b)
                    bank = 4 if isinstance(b, int) and b == 0 else 2
                    tt(gy[:, kt, :], ps[:, bank + kt, :], sz[:, kt, :], ALU.mult).then_inc(s["gated"], 1)

            def residual1(b):
                dve.wait_ge(s["ld_res"], (b + 1) * 16)
                ga = gates[:, bass.ds(b, 1), 0, :].to_broadcast([P, 2, D])
                bank = 4 if isinstance(b, int) and b == 0 else 2
                for h in range(2):
                    n = 2 * b + h
                    dve.wait_ge(s["oproj"], n + 1)
                    o = ps[:, bank + h, :].rearrange("p (c d) -> p c d", c=2)
                    if not (isinstance(b, int) and b == 0):
                        dve.wait_ge(s["x1_done"], n - 1)
                    tt(ga_out[:, h], o, ga, ALU.mult).then_inc(s["res_mul"], 1)
                for h in range(2):
                    n = 2 * b + h
                    dve.wait_ge(s["res_mul"], n + 1)
                    tt(x_tok[:, bass.ds(b * CH + 2 * h, 2), :], ga_out[:, h], u2[:, 2 * h:2 * h + 2, :],
                       ALU.add).then_inc(s["x1_done"], 1)

            def norm2(b):
                dve.wait_ge(s["ld_c"], 16)
                if not (isinstance(b, int) and b == 0):
                    dve.wait_ge(s["lnT2"], KT * b)
                dve.wait_ge(s["x1_done"], 2 * b + 2)
                normalise(x_tok[:, bass.ds(b * CH, CH), :], xn2[:], b, ("bn2", "ag2", "eps2", "rs2", "xn2_done"))

            def h2_low(b):
                for kt in range(KT):
                    dve.wait_ge(s["h2hi_done"], KT * b + kt + 1)
                    tt(h2_lo[:, kt, :], h32b[:, kt, :], h2_hi[:, kt, :].bitcast(F32),
                       ALU.subtract).then_inc(s["h2lo_done"], 1)

            def hidden(b):
                for m in range(NM):
                    n = b * NM + m
                    dve.wait_ge(s["silu_done"], n + 1)
                    dve.wait_ge(s["hlo2"], n + 1)
                    tt(hid[:, m % 2, :], ps[:, 2 + m % 2, :], silu_sb[:, m % 2, :], ALU.mult).then_inc(s["hid_done"], 1)
                    if m:
                        hidden_low(n - 1, m - 1)
                hidden_low(b * NM + NM - 1, NM - 1)

            def hidden_low(n, m):
                dve.wait_ge(s["hhi2"], n + 1)
                tt(hid_lo[:, m, :], hid[:, m % 2, :], hid_hi[:, m, :].bitcast(F32), ALU.subtract).then_inc(s["hlo2"], 1)

            def residual2(b, c):
                n = b * CH + c
                dve.wait_ge(s["down_mm"], n + 1)
                x = x_tok[:, bass.ds(n, 1), :]
                t = gb_out[:, c % 2]
                dve.wait_ge(s["x2_done"], n + 1)
                tt(t, ps[:, 4 + c % 2, 0:D].unsqueeze(1), gates[:, bass.ds(b, 1), 1, :], ALU.mult).then_inc(s["out_mul"], 1)
                dve.wait_ge(s["out_mul"], SLOTS + n + 1)
                tt(x, x, t, ALU.add).then_inc(s["x2_done"], 1)

            def ffn_step(b, normed, ahead):
                hidden(b)
                if normed:
                    h2_low(b + 1)
                residual2(b, 0)
                if ahead:
                    gate(b + 2)
                residual2(b, 1)
                if ahead:
                    residual1(b + 2)
                    norm2(b + 2)
                residual2(b, 2)
                residual2(b, 3)

            for name in ("hlo2", "out_mul", "x2_done"):
                dve.sem_inc(s[name], SLOTS)
            gate(0)
            w2_lower(2)
            w2_lower(3)
            for y_step in y_combine(NG - 1, NG * B - 1, B - 1):
                y_step()
            residual1(0)
            norm2(0)
            gate(1)
            h2_low(0)
            residual1(1)
            norm2(1)
            with dve.Fori(0, B - 2) as b:
                ffn_step(b, True, True)
            ffn_step(B - 2, True, False)
            ffn_step(B - 1, False, False)

        @block.gpsimd
        def _(pool):
            gp = nc.gpsimd

            def await_unit(name, value):
                pool.wait_ge(s[name], value)
                pool.sem_inc(s["pool_waits"], 1)

            gp.memset(minus_half[:], -0.5).then_inc(s["half_set"], 1)
            pool.wait_ge(s["half_set"], 1)

            def split_tile(g, t):
                n = (g * GT + t) * 2
                gp.tensor_copy(wg_hi[:, t], wg_raw[:, t]).then_inc(s["w_split"], 1)
                await_unit("w_split", n + 1)
                gp.tensor_tensor(wg_lo[:, t], wg_raw[:, t], wg_hi[:, t].bitcast(F32), ALU.subtract).then_inc(s["w_split"], 1)

            def inverse_root(n, eps_name, name):
                await_unit(eps_name, n + 1)
                gp.tensor_tensor(rstd[:], vareps[:], minus_half[:], ALU.pow).then_inc(s[name], 1)

            def h_low(b):
                for kt in range(KT):
                    pool.wait_ge(s["hhi_done"], KT * b + kt + 1)
                    gp.tensor_tensor(ht_lo[:, kt, b * L:(b + 1) * L], h32[:, kt, :],
                                     ht_hi[:, kt, b * L:(b + 1) * L].bitcast(F32), ALU.subtract).then_inc(s["hlo_done"], 1)

            inverse_root(0, "eps1", "rs")
            for b in range(B):
                if b + 1 < B:
                    inverse_root(b + 1, "eps1", "rs")
                h_low(b)
            pool.wait_ge(s["ld_wg"], 16)
            for t in range(GT):
                split_tile(0, t)
            pool.wait_ge(s["ld_hot"], 16)
            gp.tensor_copy(sel[:], hot_sb[:].unsqueeze(2).to_broadcast([3 * NH, NH, P])).then_inc(s["sel_done"], 1)
            pool.wait_ge(s["ld_wz"], 16)
            gp.tensor_copy(wz_hi[:], wz_raw[:]).then_inc(s["wz_split"], 1)
            pool.wait_ge(s["wz_split"], 1)
            gp.tensor_tensor(wz_lo[:], wz_raw[:], wz_hi[:].bitcast(F32), ALU.subtract).then_inc(s["wz_split"], 1)
            pool.wait_ge(s["ld_d"], 16)

            def scale_x(gq, q, b, first, second):
                if not first:
                    await_unit("state", q)
                for c in range(CH - 1):
                    n = CH - 1 - c
                    xc = x_tok[:, b * CH + c:b * CH + c + 1, bass.ds(gq * GC, GC)]
                    x4 = xc.rearrange("p t (j e) -> p t j e", j=JH).to_broadcast([P, n, JH, HD])
                    d4 = dec[:, V0[c]:V0[c] + n, b, bass.ds(gq * JH, JH)].unsqueeze(3).to_broadcast([P, n, JH, HD])
                    o4 = xds[:, b % 2, V0[c]:V0[c] + n, :].rearrange("p t (j e) -> p t j e", j=JH)
                    gp.tensor_tensor(o4, x4, d4, ALU.mult).then_inc(s["xds_done"], 1)
                if not (first or second):
                    await_unit("intra", q - 1)
                x = x_tok[:, b * CH:(b + 1) * CH, bass.ds(gq * GC, GC)]
                own = xs[:, b % 2].rearrange("p (j n) -> p j n", j=JH)[:, :, 0:P]
                own = own.rearrange("p j (c w) -> p c j w", c=CH)[:, :, :, 0:HD]
                gp.tensor_copy(own, x.rearrange("p c (j e) -> p c j e", j=JH)).then_inc(s["xs_done"], 1)
                await_unit("xs_done", q + 1)
                await_unit("xds_done", 3 * q + 3)
                x4 = x.rearrange("p c (j e) -> p c j e", j=JH)
                d4 = d_sb[:, bass.ds(gq * JH, JH)].unsqueeze(1).unsqueeze(3).to_broadcast([P, CH, JH, HD])
                gp.tensor_tensor(x4, x4, d4, ALU.mult).then_inc(s["xd_done"], 1)

            def mask(q, j):
                await_unit("exp_done", 4 * q + j + 1)
                v = decay[:, j, :].rearrange("p (c l) -> p c l", c=CH)
                gp.affine_select(out=v, in_=v, compare_op=ALU.is_ge, fill=0.0, base=0, pattern=[[0, CH], [1, P]],
                                 channel_multiplier=-1).then_inc(s["masked"], 1)

            def step(g, b, gq, first=False, split=False):
                bq = (b - 1) % B
                q = gq * B + bq
                scale_x(gq, q, bq, first, isinstance(q, int) and q == 1)
                mask(q, 0)
                mask(q, 1)
                if split:
                    await_unit("ld_wg", (g + 2) * 16)
                    for t in range(2):
                        await_unit("proj", (g * B + B - 1) * GT + t + 1)
                        split_tile(g + 1, t)
                mask(q, 2)
                mask(q, 3)
                if split:
                    for t in range(2, 4):
                        await_unit("proj", (g * B + B - 1) * GT + t + 1)
                        split_tile(g + 1, t)

            pool.wait_ge(s["dec_done"], 1)
            pool.wait_ge(s["xs_zero"], 1)
            pool.wait_ge(s["xtok_ev"], 2 * B)
            w13r = stage[:].rearrange("p (m h k n) -> p m h k n", m=NM, h=2, k=KT)
            for b in range(1, B):
                step(0, b, 0, first=(b == 1), split=(b == B - 1))
                if b == 1:
                    pool.wait_ge(s["ld_w13"], 16)
                    pool.wait_ge(s["xp_mm"], 2 * B)
                    pool.wait_ge(s["hlo_done"], KT * B)
                    pool.wait_ge(s["gate_ev"], B)
                for m in range(3 * (b - 1), min(3 * b, NM)):
                    gp.tensor_copy(w13_hi[:, m], w13r[:, m]).then_inc(s["w13_hi_done"], 1)
                    pool.wait_ge(s["w13_hi_done"], m + 1)
                    gp.tensor_tensor(w13_lo[:, m], w13r[:, m], w13_hi[:, m].bitcast(F32),
                                     ALU.subtract).then_inc(s["w13_split"], 1)
            with pool.Fori(1, NG - 1) as g:
                for b in range(B):
                    step(g, b, (g - 1 if b == 0 else g), split=(b == B - 1))
            half = [stage[:, 0:NM * D], stage[:, NM * D:]]

            def butterfly(k):
                w = 1 << k
                src = half[k % 2].rearrange("p (n e w d) -> p n e (w d)", e=2, w=w, d=D)
                dst = half[1 - k % 2].rearrange("p (n e w d) -> p n e (w d)", e=2, w=w, d=D)
                if k:
                    pool.wait_ge(s["bfly"], 2 * k)
                gp.tensor_tensor(dst[:, :, 0], src[:, :, 0], src[:, :, 1], ALU.add).then_inc(s["bfly"], 1)
                gp.tensor_tensor(dst[:, :, 1], src[:, :, 0], src[:, :, 1], ALU.subtract).then_inc(s["bfly"], 1)

            for b in range(B):
                step(NG - 1, b, NG - 2 if b == 0 else NG - 1)
                if b == 0:
                    pool.wait_ge(s["ld_w2"], 16)
                if b < 3:
                    butterfly(b)
            step(None, 0, NG - 1)

            def y_values(b):
                gp.tensor_copy(yv[:], x_tok[:, bass.ds(b * CH, CH), :]).then_inc(s["yv_done"], 1)

            inverse_root(0, "eps2", "rs2")
            inverse_root(1, "eps2", "rs2")
            with pool.Fori(2, B) as b:
                await_unit("yT_mm", KT * b)
                y_values(b)
                inverse_root(b, "eps2", "rs2")


def _layout(i):
    import numpy as np

    f = {k: np.asarray(v) for k, v in i.items()}
    w_in = f["L0_attn_W_in"]
    conv_w = f["L0_attn_conv_w"][:, 0, :]
    nb = NH * NS
    k_major = lambda w: w.T.reshape(KT, P, -1).transpose(1, 0, 2)

    def tiles(w):
        return k_major(w).reshape(P, KT, -1, P).transpose(0, 2, 1, 3)

    bt = tiles(w_in[D:D + nb]).reshape(P, NG, 2, KT, P)
    ct = tiles(w_in[D + nb:D + 2 * nb]).reshape(P, NG, 2, KT, P)
    taps = np.concatenate([conv_w, f["L0_attn_conv_b"][:, None]], axis=1)
    xc = taps[:D].reshape(2, P, TAPS + 1)
    bc = taps[D:D + nb].reshape(NG, 2, P, TAPS + 1)
    cc = taps[D + nb:].reshape(NG, 2, P, TAPS + 1)
    groups = np.concatenate([bc, cc], axis=1).reshape(NG * GT, P, TAPS + 1)
    w1, w3 = (tiles(f[n]) for n in ("L0_ffn_W1", "L0_ffn_W3"))
    n = np.arange(P)
    had = np.array([[1.0]])
    while len(had) < P:
        had = np.block([[had, had], [had, -had]])
    consts = np.stack([np.eye(P), n[:, None] <= n[None, :], n[:, None] > n[None, :], np.ones((P, P)),
                       had / np.sqrt(HID)], axis=1).astype(np.float32)
    return {
        "u": f["L0_attn_u"].reshape(B * L, D),
        "w_bc": np.concatenate([bt, ct], axis=2).transpose(1, 0, 2, 3, 4),
        "w_x": tiles(w_in[:D]),
        "w_a": k_major(w_in[2 * D + 2 * nb:]),
        "w_z": tiles(w_in[D + 2 * nb:2 * D + 2 * nb]),
        "conv": np.concatenate([groups, xc], axis=0).transpose(1, 0, 2),
        "d_rows": np.broadcast_to(f["L0_attn_D"], (P, NH)),
        "z_bias": f["L0_attn_z_bias"].reshape(2, P).T,
        "w_out": k_major(f["L0_attn_W_out"]),
        "w13": np.stack([w1, w3], axis=2).reshape(P, -1),
        "w2": f["L0_ffn_W2"].T.reshape(NM, P, D).transpose(1, 0, 2).reshape(P, -1),
        "c_t": f["L0_c"].T.reshape(KT, P, B).transpose(1, 0, 2),
        "wmod": f["L0_wmod"].reshape(KT, P, 6 * D).transpose(1, 0, 2),
        "consts": consts,
        "head_hot": np.tile(np.eye(NH, dtype=np.float32), (3, 1)),
    }


def kernel(**inputs):
    import numpy as _np
    import concourse.bacc as _bacc
    from concourse import mybir as _mybir
    from concourse.bass_utils import run_bass_kernel_spmd as _run

    nc = _bacc.Bacc("TRN2", target_bir_lowering=False, num_devices=1)
    arrays, args = {}, []
    for name, a in _layout(inputs).items():
        a = _np.ascontiguousarray(a)
        arrays[f"in_{name}"] = a
        args.append(nc.dram_tensor(f"in_{name}", a.shape, _mybir.dt.from_np(a.dtype), kind="ExternalInput").ap())
    args.append(nc.dram_tensor("out_0", (B * L, D), _mybir.dt.float32, kind="ExternalOutput").ap())
    adaln_ssm_ffn_kernel(nc, *args)
    r = _run(nc, [arrays], core_ids=[0])
    return r.results[0]["out_0"].reshape(B, L, D)
```

```python
from contextlib import ExitStack

import concourse.bass as bass
from concourse import mybir

F32 = mybir.dt.float32
F32R = mybir.dt.float32r
BF16 = mybir.dt.bfloat16
ALU = mybir.AluOpType
ACT = mybir.ActivationFunctionType

P = 128
B, L, D = 4, 512, 256
NH, HD, NS = 32, 8, 64
HID = 1024
TAPS = 4
KT = D // P
CH = L // P
TT = B * CH
JH = 4
NG = NH // JH
GT = 4
GC = JH * HD
NM = HID // P
BANK = 512
EPS = 1e-5
SLOTS = 2
PROJ_BANK = [0, 1, 4, 5]
V0 = [0, 3, 5]
NV = 6


def adaln_ssm_ffn_kernel(nc, u, w_bc, w_x, w_a, w_z, conv, d_rows, z_bias, w_out, w13, w2, c_t, wmod,
                         consts, out, sums_d, gates_d):
    with ExitStack() as ctx:
        def sb(name, shape, dt, where=ctx):
            return where.enter_context(nc.sbuf_tensor(name, shape, dt))

        def sem(name):
            return ctx.enter_context(nc.semaphore(name))

        ps = ctx.enter_context(nc.psum_tensor("ps", [P, 8, BANK], F32))

        ht_hi = sb("ht_hi", [P, KT, B * L], F32R)
        ht_lo = sb("ht_lo", [P, KT, B * L], F32R)
        x_tok = sb("x_tok", [P, TT, D], F32)
        cst = sb("cst", [P, 5, P], F32)
        ident, triu, strict, ones, hadamard = (cst[:, i, :] for i in range(5))
        wo_sb = sb("wo_sb", [P, KT, D], F32)
        wz_raw = sb("wz_raw", [P, 2, KT, P], F32)
        wz_hi = sb("wz_hi", [P, 2, KT, P], F32R)
        wz_lo = sb("wz_lo", [P, 2, KT, P], F32R)
        zb_sb = sb("zb_sb", [P, 2], F32)
        gates = sb("gates", [P, B, 2, D], F32)
        shift = sb("shift", [P, 2, KT, B], F32)
        scale1 = sb("scale1", [P, 2, KT, B], F32)
        stats = sb("stats", [P, CH, 6], F32)
        meanvar = sb("meanvar", [P, CH, 2], F32)
        vareps = sb("vareps", [P, CH], F32)
        rstd = sb("rstd", [P, CH], F32)
        minus_half = sb("minus_half", [P, CH], F32)
        stage = sb("stage", [P, 2 * NM * D], F32)

        reg_a = ExitStack()
        wmod_sb = sb("wmod_sb", [P, KT, 6 * D], F32, reg_a)
        u_sb = sb("u_sb", [P, TT, D], F32, reg_a)
        xn = sb("xn", [P, 2, CH, D], F32, reg_a)
        wx_raw = sb("wx_raw", [P, 2, KT, P], F32, reg_a)
        wx_hi = sb("wx_hi", [P, 2, KT, P], F32R, reg_a)
        wx_lo = sb("wx_lo", [P, 2, KT, P], F32R, reg_a)
        h32 = sb("h32", [P, 2, KT, L], F32, reg_a)
        reg_a.close()
        w13_hi = sb("w13_hi", [P, NM, 2, KT, P], F32R)
        w13_lo = sb("w13_lo", [P, NM, 2, KT, P], F32R)
        w2_hi = sb("w2_hi", [P, NM, D], F32R)
        w2_lo = sb("w2_lo", [P, NM, D], F32R)

        reg_b = ExitStack()
        sums = sb("sums", [P, JH, L], F32, reg_b)
        c_sb = sb("c_sb", [P, KT, B], F32, reg_b)
        c_exp = sb("c_exp", [P, KT, B], F32, reg_b)
        c_silu = sb("c_silu", [P, KT, B], F32, reg_b)
        p_tok = sb("p_tok", [P, TT, NH], F32, reg_b)
        e_tok = sb("e_tok", [P, TT, NH], F32, reg_b)
        dec = sb("dec", [P, NV, B, NH], F32, reg_b)
        conv_sb = sb("conv_sb", [P, NG * GT + 2, TAPS + 1], F32, reg_b)
        d_sb = sb("d_sb", [P, NH], F32, reg_b)
        wg_raw = sb("wg_raw", [P, GT, KT, P], F32, reg_b)
        wg_hi = sb("wg_hi", [P, GT, KT, P], F32R, reg_b)
        wg_lo = sb("wg_lo", [P, GT, KT, P], F32R, reg_b)
        cw_act = sb("cw_act", [P, GT, 2], F32, reg_b)
        cw_dve = sb("cw_dve", [P, GT, 3], F32, reg_b)
        p_slot = sb("p_slot", [P, TT, JH], F32, reg_b)
        acc = sb("acc", [P, 2, GT, L], F32, reg_b)
        decay = sb("decay", [P, JH, L], F32, reg_b)
        reg_c = ExitStack()
        a_abs = sb("a_abs", [P, TT * NH], F32, reg_c)
        a_exp = sb("a_exp", [P, TT * NH], F32, reg_c)
        sums_t = sb("sums_t", [P, L], F32, reg_c)
        wa_sb = sb("wa_sb", [P, KT, NH], F32, reg_c)
        sp_a = sb("sp_a", [P, B, CH, NH], F32, reg_c)
        reg_c.close()
        mix = sb("mix", [P, JH, L], F32, reg_b)
        b_tok = sb("b_tok", [P, 2, 3 * P], F32, reg_b)
        yt_sb = sb("yt_sb", [2 * GC, L], F32, reg_b)
        xds = sb("xds", [P, 2, NV, GC], F32, reg_b)
        st_sb = sb("st_sb", [P, 2, 3, GC], F32, reg_b)
        xs = sb("xs", [P, 2, JH * (P + HD)], F32, reg_b)
        y_off = sb("y_off", [P, 3, GC], F32, reg_b)
        reg_b.close()
        hid_hi = sb("hid_hi", [P, NM, L], F32R)
        yv = sb("yv", [P, CH, D], F32)
        u2 = sb("u2", [P, CH, D], F32)
        sz = sb("sz", [P, KT, L], F32)
        gy = sb("gy", [P, KT, L], F32)
        hid_lo = sb("hid_lo", [P, NM, L], F32R)
        hid = sb("hid", [P, 2, L], F32)
        silu_sb = sb("silu_sb", [P, 2, L], F32)
        xn2 = sb("xn2", [P, CH, D], F32)
        h32b = sb("h32b", [P, KT, L], F32)
        h2_hi = sb("h2_hi", [P, KT, L], F32R)
        h2_lo = sb("h2_lo", [P, KT, L], F32R)
        ga_out = stage[:, 0:4 * D].rearrange("p (n c d) -> p n c d", n=2, c=2)
        gb_out = stage[:, 4 * D:6 * D].rearrange("p (n c d) -> p n c d", n=2, c=1)

        names = """
        ld_c ld_wmod ld_wmod2 ld_u0 ld_u1 ld_u2 ld_u3 ld_cst ld_wx ld_wa ld_conv ld_sum0 ld_sum1 ld_sum2 ld_sum3
        st_sums ld_d ld_wg ld_wz ld_zb ld_wo ld_w13 ld_w2 ld_res st_out c_exp_done c_one c_rec c_silu_done
        mod_mm mod_ev gate_mm gate_abs gate_sign gate_ev st_gates ld_gates bnst bnag eps1 rs half_set xn_done
        lnT_mm h32_done hhi_done hlo_done wx_split wz_split xp_mm xtap xtaps xT_mm xtok_ev a_mm abs_done
        aexp_done aln_done sp_done ptok_mm dk_mm e_done dec_done p_copy sumsT_mm sumsT_ev st_zero w_split cwa
        cwd p_sl pool_waits dve_waits pe_waits proj tap0 taps bt bt_ev diff_done exp_done score mixed state
        st_copy masked xds_done xs_done xd_done inter intra yt_ev y_tok xs_zero yoff_done y_mid y_done
        w13_hi_done w13_split bfly w2_mm w2_hi_done w2_split yv_done z_mm yT_mm silu_z gated oproj res_mul
        x1_done bn2 ag2 eps2 rs2 xn2_done lnT2 h32b_done h2hi_done h2lo_done up_mm silu_done hid_done hhi2 hlo2
        down_mm out_mul x2_done
        """.split()
        s = {n: sem(n) for n in names}

        block = ctx.enter_context(nc.Block())

        @block.sync
        def _(sp):
            def load(dst, src, name):
                sp.dma_start(dst, src).then_inc(s[name], 16)

            u_b = u.rearrange("(b c p) d -> b p c d", b=B, p=P)
            out_b = out.rearrange("(b c p) d -> b p c d", b=B, p=P)
            load(c_sb[:], c_t, "ld_c")
            load(u_sb[:, 0:CH, :], u_b[0], "ld_u0")
            load(cst[:], consts, "ld_cst")
            load(wmod_sb[:, :, 0:2 * D], wmod[:, :, 0:2 * D], "ld_wmod")
            load(wx_raw[:], w_x, "ld_wx")
            load(u_sb[:, CH:2 * CH, :], u_b[1], "ld_u1")
            load(wa_sb[:], w_a, "ld_wa")
            load(u_sb[:, 2 * CH:3 * CH, :], u_b[2], "ld_u2")
            load(conv_sb[:], conv, "ld_conv")
            load(u_sb[:, 3 * CH:, :], u_b[3], "ld_u3")
            load(wg_raw[:], w_bc[0], "ld_wg")
            load(wmod_sb[:, :, 2 * D:], wmod[:, :, 2 * D:], "ld_wmod2")
            load(d_sb[:], d_rows, "ld_d")
            load(wz_raw[:], w_z, "ld_wz")
            load(zb_sb[:], z_bias, "ld_zb")
            load(wo_sb[:], w_out, "ld_wo")
            load(stage[:], w13, "ld_w13")

            sp.wait_ge(s["sumsT_ev"], 1)
            for c in range(CH):
                sp.dma_start(sums_d.rearrange("(b h) (c l) -> c h b l", b=B, c=CH)[c],
                             sums_t[c * NH:(c + 1) * NH, :].rearrange("h (b l) -> h b l", b=B)).then_inc(s["st_sums"], 16)
            sp.wait_ge(s["st_sums"], 16 * CH)

            def load_sums(g, b, first=False):
                q = g * B + b
                for j in range(JH):
                    if not first:
                        sp.wait_ge(s["diff_done"], 4 * q + j - 3)
                    row = sums_d[bass.ds(b * NH + g * JH + j, 1), :]
                    sp.dma_start(sums[:, j, :], row.to_broadcast([P, L])).then_inc(s[f"ld_sum{j}"], 16)

            def load_group(g):
                sp.wait_ge(s["w_split"], g * (2 * GT))
                sp.dma_start(wg_raw[:], w_bc[bass.ds(g, 1)].rearrange("a p t k m -> p (a t) k m")).then_inc(s["ld_wg"], 16)

            load_sums(0, 0, first=True)
            load_group(1)
            sp.wait_ge(s["gate_ev"], 1)
            sp.dma_start(gates_d, xn[0:B, 0, 0:2, :].rearrange("b k d -> b (k d)")).then_inc(s["st_gates"], 16)
            sp.wait_ge(s["st_gates"], 16)
            for b in range(B):
                sp.dma_start(gates[:, b].rearrange("p k d -> p (k d)"),
                             gates_d[b:b + 1, :].to_broadcast([P, 2 * D])).then_inc(s["ld_gates"], 16)
            for b in range(1, B):
                load_sums(0, b)
            with sp.Fori(1, NG - 1) as g:
                for b in range(B):
                    load_sums(g, b)
                    if b == 1:
                        load_group(g + 1)
            for b in range(B):
                load_sums(NG - 1, b)
                if b == 0:
                    sp.wait_ge(s["w13_split"], NM)
                    load(stage[:, 0:NM * D], w2, "ld_w2")
            sp.wait_ge(s["xd_done"], NG * B)
            sp.wait_ge(s["proj"], NG * B * GT)
            for b in range(B):
                if b:
                    sp.wait_ge(s["x1_done"], 2 * b)
                load(u2[:], u_b[b], "ld_res")
            for b in range(B - 1):
                sp.wait_ge(s["x2_done"], SLOTS + CH * (b + 1))
                sp.dma_start(out_b[b], x_tok[:, b * CH:(b + 1) * CH, :]).then_inc(s["st_out"], 16)
            for c in range(CH):
                t = (B - 1) * CH + c
                sp.wait_ge(s["x2_done"], SLOTS + t + 1)
                sp.dma_start(out_b[B - 1][:, c, :], x_tok[:, t, :]).then_inc(s["st_out"], 16)
            sp.wait_ge(s["st_out"], 16 * (B - 1 + CH))

        @block.tensor
        def _(pe):
            mm = nc.tensor.matmul

            def split_mm(o, w_hi, w_lo, x_hi, x_lo, first, last):
                mm(o, w_hi, x_hi, start=first, stop=False)
                mm(o, w_hi, x_lo, start=False, stop=False)
                return mm(o, w_lo, x_hi, start=False, stop=last)

            def modulation(kinds, bank):
                pe.wait_ge(s["c_silu_done"], 1)
                for k, kind in enumerate(kinds):
                    for m in range(KT):
                        o = ps[:, bank, (2 * k + m) * B:(2 * k + m + 1) * B]
                        for kt in range(KT):
                            i = mm(o, wmod_sb[:, kt, kind * D + m * P:kind * D + (m + 1) * P], c_silu[:, kt, :],
                                   start=(kt == 0), stop=(kt == KT - 1))
                i.then_inc(s["mod_mm"], 1)

            def norm_transposes(b):
                pe.wait_ge(s["xn_done"], CH * (b + 1))
                if b:
                    pe.wait_ge(s["h32_done"], KT * b)
                for c in range(CH):
                    for kt in range(KT):
                        i = nc.tensor.transpose(ps[:, 2 + kt, c * P:(c + 1) * P],
                                                xn[:, b % 2, c, kt * P:(kt + 1) * P], ident)
                i.then_inc(s["lnT_mm"], 1)

            def gate_rows():
                pe.wait_ge(s["h32_done"], KT * B)
                for k, kind in enumerate((2, 5)):
                    for kt in range(KT):
                        i = mm(ps[0:B, 2, k * D:(k + 1) * D], c_silu[:, kt, :],
                               wmod_sb[:, kt, kind * D:(kind + 1) * D], start=(kt == 0), stop=(kt == KT - 1))
                i.then_inc(s["gate_mm"], 1)

            def x_project(b):
                pe.wait_ge(s["hlo_done"], KT * (b + 1))
                for xt in range(2):
                    n = 2 * b + xt
                    if n >= 2:
                        pe.wait_ge(s["xtaps"], 3 * (n - 1))
                    for kt in range(KT):
                        i = split_mm(ps[:, xt, :], wx_hi[:, xt, kt, :], wx_lo[:, xt, kt, :],
                                     ht_hi[:, kt, b * L:(b + 1) * L], ht_lo[:, kt, b * L:(b + 1) * L],
                                     kt == 0, kt == KT - 1)
                    i.then_inc(s["xp_mm"], 1)

            def a_project(b):
                pe.wait_ge(s["h32_done"], KT * (b + 1))
                for c in range(CH):
                    t = b * CH + c
                    for kt in range(KT):
                        i = mm(ps[:, 6, t * NH:(t + 1) * NH], h32[:, b % 2, kt, c * P:(c + 1) * P], wa_sb[:, kt, :],
                               start=(kt == 0), stop=(kt == KT - 1))
                i.then_inc(s["a_mm"], 1)

            def x_transposes(b):
                for xt in range(2):
                    n = 2 * b + xt
                    pe.wait_ge(s["xtaps"], 3 * (n + 1))
                    if n >= 2:
                        pe.wait_ge(s["xtok_ev"], n - 1)
                    for c in range(CH):
                        i = nc.tensor.transpose(ps[:, 4 + xt, c * P:(c + 1) * P],
                                                acc[:, n // GT, n % GT, c * P:(c + 1) * P], ident)
                    i.then_inc(s["xT_mm"], 1)

            def proj(g, b, t):
                n = (g * B + b) * GT + t
                if not (isinstance(g, int) and g == 0 and b == 0):
                    pe.wait_ge(s["taps"], (n - GT + 1) * 3)
                if b == 0:
                    pe.wait_ge(s["w_split"], (g * GT + t) * 2 + 2)
                for kt in range(KT):
                    i = split_mm(ps[:, PROJ_BANK[t], :], wg_hi[:, t, kt, :], wg_lo[:, t, kt, :],
                                 ht_hi[:, kt, b * L:(b + 1) * L], ht_lo[:, kt, b * L:(b + 1) * L],
                                 kt == 0, kt == KT - 1)
                i.then_inc(s["proj"], 1)

            pe.wait_ge(s["ld_cst"], 16)
            norm_transposes(0)
            pe.wait_ge(s["ld_wmod"], 16)
            modulation((0, 1), 0)
            pe.wait_ge(s["mod_ev"], 2)
            pe.wait_ge(s["wx_split"], 2)
            pe.wait_ge(s["ld_wa"], 16)
            for b in range(B):
                if b + 1 < B:
                    norm_transposes(b + 1)
                a_project(b)
                x_project(b)
                if b:
                    x_transposes(b - 1)
            x_transposes(B - 1)
            pe.wait_ge(s["xtaps"], 3 * 2 * B)
            proj(0, 0, 0)
            pe.wait_ge(s["ld_wmod2"], 16)
            modulation((3, 4), 7)

            pe.wait_ge(s["sp_done"], 1)
            pe.wait_ge(s["mod_ev"], 4)
            mm(ps[:, 7, :], triu, sp_a[:].rearrange("p b c h -> p (b c h)"), start=True,
               stop=True).then_inc(s["ptok_mm"], 1)
            pe.wait_ge(s["xtok_ev"], 2 * B)
            for c in range(CH - 1):
                for t in range(CH - 1 - c):
                    v = V0[c] + t
                    o = ps[:, 4 + v // 3, (v % 3) * B * NH:(v % 3 + 1) * B * NH]
                    i = mm(o, strict, sp_a[:, :, c, :], start=True, stop=(t == 0))
                    for k in range(t):
                        i = mm(o, ones, sp_a[:, :, c + 1 + k, :], start=False, stop=(k == t - 1))
            i.then_inc(s["dk_mm"], 1)
            def b_transposes(q, b, p, first):
                pe.wait_ge(s["taps"], 12 * q + 3 * (p + 1))
                if not first or p:
                    pe.wait_ge(s["bt_ev"], 2 * q + p)
                for c in range(CH - 1):
                    i = nc.tensor.transpose(ps[:, 6, c * P:(c + 1) * P],
                                            acc[:, b % 2, p, c * P:(c + 1) * P], ident)
                i.then_inc(s["bt"], 1)

            def scores(q, b, p, first):
                pe.wait_ge(s["taps"], 12 * q + 3 * (3 + p))
                if not first or p:
                    pe.wait_ge(s["mixed"], 4 * q + 2 * p)
                else:
                    pe.wait_ge(s["gate_ev"], 1)
                for c in range(CH):
                    for a in range(2):
                        i = mm(ps[:, 2 + a, c * P:(c + 1) * P],
                               acc[NS * a:NS * (a + 1), b % 2, p, c * P:(c + 1) * P],
                               acc[NS * a:NS * (a + 1), b % 2, 2 + p, c * P:(c + 1) * P],
                               start=True, stop=True)
                        if c == CH - 1:
                            i.then_inc(s["score"], 1)

            def states(q, b):
                pe.wait_ge(s["bt_ev"], 2 * q + 2)
                pe.wait_ge(s["xds_done"], 3 * q + 3)
                for p in range(2):
                    for c in range(CH - 1):
                        n = CH - 1 - c
                        o = ps[:, 6, 3 * P + p * 48 + c * 16:3 * P + (p + 1) * 48]
                        i = mm(o, b_tok[:, p, c * P:(c + 1) * P],
                               xds[:, b % 2, V0[c]:V0[c] + n, 16 * p:16 * (p + 1)],
                               start=(c == 0), stop=(c == CH - 2))
                i.then_inc(s["state"], 1)

            def inter(q, b, first):
                pe.wait_ge(s["st_copy"], 2 * q + 2)
                if not first:
                    pe.wait_ge(s["yoff_done"], q)
                    pe.wait_ge(s["y_mid"], q)
                for c in range(1, CH):
                    for p in range(2):
                        i = mm(ps[GC:2 * GC, 7, c * P:(c + 1) * P], st_sb[:, p, c - 1, :],
                               acc[:, b % 2, 2 + p, c * P:(c + 1) * P], start=(p == 0), stop=(p == 1))
                i.then_inc(s["inter"], 1)

            def intra(q, b):
                pe.wait_ge(s["xs_done"], q + 1)
                pe.wait_ge(s["mixed"], 4 * q + 4)
                for c in range(CH):
                    for j in range(JH):
                        k = j * P + c * GC
                        i = mm(ps[0:GC, 7, c * P:(c + 1) * P], xs[:, b % 2, k:k + GC],
                               mix[:, j, c * P:(c + 1) * P], start=(j == 0), stop=(j == JH - 1))
                i.then_inc(s["intra"], 1)

            def y_transposes(q):
                pe.wait_ge(s["yt_ev"], 2 * q + 2)
                pe.sem_inc(s["pe_waits"], 1)
                for c in range(CH):
                    rows = 2 * GC if c else GC
                    i = nc.tensor.transpose(ps[:, 7, c * 2 * GC:c * 2 * GC + rows],
                                            yt_sb[0:rows, c * P:(c + 1) * P], cst[0:rows, 0, 0:rows])
                i.then_inc(s["y_tok"], 1)

            def w2_transform(n):
                if n < 2:
                    pe.wait_ge(s["taps"], 3 * (NG * B * GT - GT + n + 1))
                else:
                    pe.wait_ge(s["mixed"], NG * B * JH)
                mm(ps[:, n, :], hadamard, stage[:, NM * D + n * BANK:NM * D + (n + 1) * BANK], start=True,
                   stop=True).then_inc(s["w2_mm"], 1)

            def z_project(b, zt):
                if not isinstance(b, int):
                    pe.wait_ge(s["hid_done"], NM * (b - 1))
                elif b == 0:
                    pe.wait_ge(s["w2_split"], zt + 1)
                else:
                    pe.wait_ge(s["silu_z"], zt + 1)
                for kt in range(KT):
                    x0 = ht_hi[:, kt, bass.ds(b * L, L)]
                    x1 = ht_lo[:, kt, bass.ds(b * L, L)]
                    i = split_mm(ps[:, zt, :], wz_hi[:, zt, kt, :], wz_lo[:, zt, kt, :], x0, x1, kt == 0, kt == KT - 1)
                i.then_inc(s["z_mm"], 1)

            def step(g, b, gq=None, gr=None):
                bq, br = (b - 1) % B, (b - 2) % B
                q = gq * B + bq if gq is not None else None
                r = gr * B + br if gr is not None else None
                first = r is None
                project = g is not None
                if not project:
                    pe.wait_ge(s["bfly"], 6)
                    pe.wait_ge(s["wz_split"], 2)
                if q is not None:
                    b_transposes(q, bq, 0, first)
                if project:
                    proj(g, b, 0)
                else:
                    w2_transform(0)
                if r is not None:
                    intra(r, br)
                if q is not None:
                    scores(q, bq, 0, first)
                    b_transposes(q, bq, 1, first)
                if project:
                    proj(g, b, 1)
                else:
                    w2_transform(1)
                if r is not None:
                    y_transposes(r)
                if q is not None:
                    scores(q, bq, 1, first)
                if project:
                    proj(g, b, 2)
                else:
                    z_project(0, 0)
                if q is not None:
                    states(q, bq)
                if project:
                    proj(g, b, 3)
                else:
                    z_project(0, 1)
                if q is not None:
                    inter(q, bq, first)

            pe.wait_ge(s["p_copy"], 1)
            for b in range(B):
                i = nc.tensor.transpose(ps[:, 6, b * P:(b + 1) * P],
                                        p_tok[:, b * CH:(b + 1) * CH, :].rearrange("p c h -> p (c h)"), ident)
            i.then_inc(s["sumsT_mm"], 1)
            proj(0, 0, 1)
            gate_rows()
            pe.wait_ge(s["dec_done"], 1)
            proj(0, 0, 2)
            proj(0, 0, 3)
            pe.wait_ge(s["sumsT_ev"], 1)
            pe.wait_ge(s["e_done"], 1)
            pe.wait_ge(s["dec_done"], 1)
            pe.wait_ge(s["p_copy"], 1)
            pe.wait_ge(s["st_zero"], 1)
            pe.wait_ge(s["xs_zero"], 1)
            for b in range(1, B):
                step(0, b, gq=0, gr=(None if b == 1 else 0))
            with pe.Fori(1, NG) as g:
                for b in range(B):
                    step(g, b, gq=(g - 1 if b == 0 else g), gr=(g - 1 if b < 2 else g))
            step(None, 0, gq=NG - 1, gr=NG - 1)
            intra(NG * B - 1, B - 1)

            def yT_transposes(b, bank):
                if isinstance(b, int):
                    src = x_tok[:, b * CH:(b + 1) * CH, :]
                    pe.wait_ge(s["y_done"], (NG - 1) * B + b + 1)
                else:
                    src = yv
                    pe.wait_ge(s["yv_done"], b - 1)
                    pe.wait_ge(s["x1_done"], 2 * b)
                for kt in range(KT):
                    for c in range(CH):
                        i = nc.tensor.transpose(ps[:, bank + kt, c * P:(c + 1) * P], src[:, c, kt * P:(kt + 1) * P], ident)
                    i.then_inc(s["yT_mm"], 1)

            def out_project(b, bank):
                pe.wait_ge(s["gated"], KT * (b + 1))
                for c in range(CH):
                    for kt in range(KT):
                        i = mm(ps[:, bank + c // 2, (c % 2) * D:(c % 2 + 1) * D], gy[:, kt, c * P:(c + 1) * P],
                               wo_sb[:, kt, :], start=(kt == 0), stop=(kt == KT - 1))
                    if c % 2:
                        i.then_inc(s["oproj"], 1)

            def norm2_transposes(b):
                pe.wait_ge(s["xn2_done"], CH * (b + 1))
                for kt in range(KT):
                    for c in range(CH):
                        i = nc.tensor.transpose(ps[:, 6 + kt, c * P:(c + 1) * P], xn2[:, c, kt * P:(kt + 1) * P], ident)
                    i.then_inc(s["lnT2"], 1)

            def up(b, fronts):
                pe.wait_ge(s["h2lo_done"], KT * (b + 1))
                pe.wait_ge(s["silu_z"], KT * fronts)
                pe.wait_ge(s["x1_done"], 2 * fronts)
                for m in range(NM):
                    if m >= 2:
                        pe.wait_ge(s["hid_done"], b * NM + m - 1)
                    for half in range(2):
                        for kt in range(KT):
                            i = split_mm(ps[:, 2 * half + m % 2, :], w13_hi[:, m, half, kt, :],
                                         w13_lo[:, m, half, kt, :], h2_hi[:, kt, :], h2_lo[:, kt, :],
                                         kt == 0, kt == KT - 1)
                    i.then_inc(s["up_mm"], 1)

            def down(b, c):
                pe.wait_ge(s["out_mul"], b * CH + c + 1)
                for m in range(NM):
                    if c == 0:
                        pe.wait_ge(s["hlo2"], SLOTS + NM * b + m + 1)
                    i = split_mm(ps[:, 4 + c % 2, 0:D], hid_hi[:, m, c * P:(c + 1) * P], hid_lo[:, m, c * P:(c + 1) * P],
                                 w2_hi[:, m, :], w2_lo[:, m, :], m == 0, m == NM - 1)
                i.then_inc(s["down_mm"], 1)

            def ffn_step(b, normed, ahead):
                up(b, b + 2 if normed else B)
                if normed:
                    norm2_transposes(b + 1)
                if ahead:
                    z_project(b + 2, 0)
                    z_project(b + 2, 1)
                down(b, 0)
                if ahead:
                    yT_transposes(b + 2, 2)
                down(b, 1)
                if ahead:
                    out_project(b + 2, 2)
                down(b, 2)
                down(b, 3)

            pe.wait_ge(s["taps"], NG * B * GT * 3)
            yT_transposes(0, 4)
            w2_transform(2)
            w2_transform(3)
            y_transposes(NG * B - 1)
            pe.wait_ge(s["ld_wo"], 16)
            out_project(0, 4)
            z_project(1, 0)
            z_project(1, 1)
            pe.wait_ge(s["w2_split"], 4)
            yT_transposes(1, 2)
            out_project(1, 2)
            pe.wait_ge(s["y_done"], NG * B)
            norm2_transposes(0)
            with pe.Fori(0, B - 2) as b:
                ffn_step(b, True, True)
            ffn_step(B - 2, True, False)
            ffn_step(B - 1, False, False)

        @block.scalar
        def _(act):
            af = nc.scalar.activation

            act.wait_ge(s["ld_c"], 16)
            af(c_exp[:], c_sb[:], ACT.Exp, scale=-1.0).then_inc(s["c_exp_done"], 1)

            def h_parts(b):
                act.wait_ge(s["lnT_mm"], b + 1)
                for kt in range(KT):
                    n = KT * b + kt
                    if b >= 2:
                        act.wait_ge(s["hlo_done"], n - 3)
                        act.wait_ge(s["a_mm"], b - 1)
                    af(h32[:, b % 2, kt, :], ps[:, 2 + kt, :], ACT.Identity, bias=shift[:, 0, kt, b:b + 1],
                       scale=scale1[:, 0, kt, b:b + 1]).then_inc(s["h32_done"], 1)
                for kt in range(KT):
                    act.wait_ge(s["h32_done"], KT * b + kt + 1)
                    nc.scalar.copy(ht_hi[:, kt, b * L:(b + 1) * L], h32[:, b % 2, kt, :]).then_inc(s["hhi_done"], 1)

            def x_tap(b):
                for xt in range(2):
                    n = 2 * b + xt
                    act.wait_ge(s["xp_mm"], n + 1)
                    w = conv_sb[:, NG * GT + xt, :]
                    af(acc[:, n // GT, n % GT, :], ps[:, xt, :], ACT.Identity, bias=w[:, TAPS:TAPS + 1],
                       scale=w[:, TAPS - 1:TAPS]).then_inc(s["xtap"], 1)

            def x_evacuate(b):
                for xt in range(2):
                    n = 2 * b + xt
                    act.wait_ge(s["xT_mm"], n + 1)
                    nc.scalar.copy(x_tok[:, b * CH:(b + 1) * CH, xt * P:(xt + 1) * P],
                                   ps[:, 4 + xt, :].rearrange("p (c m) -> p c m", c=CH)).then_inc(s["xtok_ev"], 1)

            act.wait_ge(s["mod_ev"], 2)
            act.wait_ge(s["ld_conv"], 16)
            h_parts(0)
            for b in range(B):
                if b + 1 < B:
                    h_parts(b + 1)
                x_tap(b)
                if b:
                    x_evacuate(b - 1)

            act.wait_ge(s["a_mm"], B)
            af(a_abs[:], ps[:, 6, :], ACT.Abs).then_inc(s["abs_done"], 1)
            act.wait_ge(s["abs_done"], 1)
            af(a_exp[:], a_abs[:], ACT.Exp, scale=-1.0).then_inc(s["aexp_done"], 1)
            act.wait_ge(s["aexp_done"], 1)
            af(a_exp[:], a_exp[:], ACT.Ln, bias=1.0).then_inc(s["aln_done"], 1)
            x_evacuate(B - 1)
            def last_tap(g, b, t):
                n = (g * B + b) * GT + t
                act.wait_ge(s["proj"], n + 1)
                af(acc[:, b % 2, t, :], ps[:, PROJ_BANK[t], :], ACT.Identity, bias=cw_act[:, t, 1:2],
                   scale=cw_act[:, t, 0:1]).then_inc(s["tap0"], 1)

            nc.scalar.copy(cw_act[:], conv_sb[:, 0:GT, TAPS - 1:TAPS + 1]).then_inc(s["cwa"], 1)
            act.wait_ge(s["xT_mm"], 2 * B)
            act.wait_ge(s["cwa"], 1)
            last_tap(0, 0, 0)
            act.wait_ge(s["p_copy"], 1)
            af(e_tok[:].rearrange("p t h -> p (t h)"), ps[:, 7, :], ACT.Exp, scale=-1.0).then_inc(s["e_done"], 1)
            act.wait_ge(s["dk_mm"], 1)
            for k in range(2):
                i = af(dec[:, 3 * k:3 * k + 3, :, :].rearrange("p v b h -> p (v b h)"), ps[:, 4 + k, 0:3 * B * NH],
                       ACT.Exp, scale=-1.0)
            i.then_inc(s["dec_done"], 1)
            act.wait_ge(s["sumsT_mm"], 1)
            nc.scalar.copy(sums_t[:], ps[:, 6, :]).then_inc(s["sumsT_ev"], 1)

            def b_evacuate(q, p):
                act.wait_ge(s["bt"], 2 * q + p + 1)
                nc.scalar.copy(b_tok[:, p, :], ps[:, 6, 0:3 * P]).then_inc(s["bt_ev"], 1)

            def decays(q, b, j, first):
                act.wait_ge(s[f"ld_sum{j}"], 16 * (q + 1))
                if not first:
                    act.wait_ge(s["mixed"], 4 * q + j - 3)
                for c in range(CH):
                    i = af(decay[:, j, c * P:(c + 1) * P], sums[:, j, c * P:(c + 1) * P], ACT.Relu,
                           bias=p_slot[:, b * CH + c, j:j + 1])
                i.then_inc(s["diff_done"], 1)
                act.wait_ge(s["diff_done"], 4 * q + j + 1)
                af(decay[:, j, :], decay[:, j, :], ACT.Exp, scale=-1.0).then_inc(s["exp_done"], 1)

            def inter_evacuate(r, start):
                act.wait_ge(s["inter"], r + 1)
                if not start:
                    act.wait_ge(s["y_tok"], r)
                nc.scalar.copy(yt_sb[GC:2 * GC, P:], ps[GC:2 * GC, 7, P:]).then_inc(s["yt_ev"], 1)

            def intra_evacuate(r):
                act.wait_ge(s["intra"], r + 1)
                nc.scalar.copy(yt_sb[0:GC, :], ps[0:GC, 7, :]).then_inc(s["yt_ev"], 1)

            def w2_upper(n):
                act.wait_ge(s["w2_mm"], n + 1)
                nc.scalar.copy(w2_hi[:, 2 * n:2 * n + 2, :].rearrange("p m d -> p (m d)"),
                               ps[:, n, :]).then_inc(s["w2_hi_done"], 1)

            def step(g, b, attend=True, project=True, gq=None, gr=None, first=False):
                bq = (b - 1) % B
                q = gq * B + bq if attend else None
                first_r = isinstance(gr, int) and gr == 0 and b == 2
                if project and b == 0:
                    if attend:
                        act.wait_ge(s["tap0"], g * (GT * B))
                    nc.scalar.copy(cw_act[:], conv_sb[:, bass.ds(g * GT, GT), TAPS - 1:TAPS + 1]).then_inc(s["cwa"], 1)
                if project and b == 1:
                    act.wait_ge(s["exp_done"], g * 4 * B) if not (isinstance(g, int) and g == 0) else None
                    nc.scalar.mul(p_slot[:], p_tok[:, :, bass.ds(g * JH, JH)], -1.0).then_inc(s["p_sl"], 1)
                    act.wait_ge(s["p_sl"], g + 1)
                if attend:
                    b_evacuate(q, 0)
                    decays(q, bq, 0, first)
                if gr is not None:
                    inter_evacuate(gr * B + (b - 2) % B, first_r)
                if project:
                    if b == 0:
                        act.wait_ge(s["cwa"], g + 1)
                    last_tap(g, b, 0)
                else:
                    w2_upper(0)
                if attend:
                    decays(q, bq, 1, first)
                if gr is not None:
                    intra_evacuate(gr * B + (b - 2) % B)
                if attend:
                    decays(q, bq, 2, first)
                    b_evacuate(q, 1)
                if project:
                    last_tap(g, b, 1)
                else:
                    w2_upper(1)
                if attend:
                    decays(q, bq, 3, first)
                if project:
                    last_tap(g, b, 2)
                    last_tap(g, b, 3)

            last_tap(0, 0, 1)
            act.wait_ge(s["gate_mm"], 1)
            act.wait_ge(s["lnT_mm"], B)
            af(xn[0:B, 0, 0:2, :].rearrange("b k d -> b (k d)"), ps[0:B, 2, :], ACT.Abs).then_inc(s["gate_abs"], 1)
            last_tap(0, 0, 2)
            last_tap(0, 0, 3)
            act.wait_ge(s["st_sums"], 16 * CH)
            for b in range(1, B):
                step(0, b, gq=0, gr=(None if b == 1 else 0), first=(b == 1))
            with act.Fori(1, NG) as g:
                for b in range(B):
                    step(g, b, gq=(g - 1 if b == 0 else g), gr=(g - 1 if b < 2 else g))
            step(None, 0, gq=NG - 1, gr=NG - 1, project=False)

            def silu_gate(b):
                for zt in range(2):
                    act.wait_ge(s["z_mm"], 2 * b + zt + 1)
                    if not (isinstance(b, int) and b == 0):
                        act.wait_ge(s["gated"], KT * (b - 1) + zt + 1)
                    af(sz[:, zt, :], ps[:, zt, :], ACT.Silu, bias=zb_sb[:, zt:zt + 1]).then_inc(s["silu_z"], 1)

            def h2_parts(b):
                for kt in range(KT):
                    act.wait_ge(s["lnT2"], KT * b + kt + 1)
                    af(h32b[:, kt, :], ps[:, 6 + kt, :], ACT.Identity, bias=shift[:, 1, kt, bass.ds(b, 1)],
                       scale=scale1[:, 1, kt, bass.ds(b, 1)]).then_inc(s["h32b_done"], 1)
                for kt in range(KT):
                    act.wait_ge(s["h32b_done"], KT * b + kt + 1)
                    nc.scalar.copy(h2_hi[:, kt, :], h32b[:, kt, :]).then_inc(s["h2hi_done"], 1)

            def hidden(b):
                for m in range(NM):
                    n = b * NM + m
                    act.wait_ge(s["up_mm"], n + 1)
                    af(silu_sb[:, m % 2, :], ps[:, m % 2, :], ACT.Silu).then_inc(s["silu_done"], 1)
                    act.wait_ge(s["hid_done"], n + 1)
                    nc.scalar.copy(hid_hi[:, m, :], hid[:, m % 2, :]).then_inc(s["hhi2"], 1)

            act.wait_ge(s["ld_zb"], 16)
            inter_evacuate(NG * B - 1, False)
            silu_gate(0)
            intra_evacuate(NG * B - 1)
            w2_upper(2)
            w2_upper(3)
            silu_gate(1)
            h2_parts(0)
            with act.Fori(0, B - 2) as b:
                hidden(b)
                h2_parts(b + 1)
                silu_gate(b + 2)
            hidden(B - 2)
            h2_parts(B - 1)
            hidden(B - 1)

        @block.vector
        def _(dve):
            ts = nc.vector.tensor_scalar
            tt = nc.vector.tensor_tensor
            stt = nc.vector.scalar_tensor_tensor

            dve.wait_ge(s["c_exp_done"], 1)
            ts(c_exp[:], c_exp[:], 1.0, None, ALU.add).then_inc(s["c_one"], 1)
            dve.wait_ge(s["c_one"], 1)
            nc.vector.reciprocal(c_exp[:], c_exp[:]).then_inc(s["c_rec"], 1)
            dve.wait_ge(s["c_rec"], 1)
            tt(c_silu[:], c_sb[:], c_exp[:], ALU.mult).then_inc(s["c_silu_done"], 1)
            dve.wait_ge(s["c_silu_done"], 1)
            def statistics(src, n, names):
                st, ag, ep, rs, done = names
                for c in range(CH):
                    nc.vector.bn_stats(stats[:, c, :], src[:, c, :]).then_inc(s[st], 1)
                for c in range(CH):
                    dve.wait_ge(s[st], n * CH + c + 1)
                    dve.sem_inc(s["dve_waits"], 1)
                    nc.vector.bn_aggr(meanvar[:, c, :], stats[:, c, :]).then_inc(s[ag], 1)
                dve.wait_ge(s[ag], n * CH + CH)
                ts(vareps[:], meanvar[:, :, 1], EPS, None, ALU.add).then_inc(s[ep], 1)

            def normalise(src, dst, n, names):
                st, ag, ep, rs, done = names
                dve.wait_ge(s[rs], n + 1)
                for c in range(CH):
                    ts(dst[:, c, :], src[:, c, :], meanvar[:, c, 0:1], rstd[:, c:c + 1], ALU.subtract,
                       ALU.mult).then_inc(s[done], 1)

            norm1_names = ("bnst", "bnag", "eps1", "rs", "xn_done")
            norm2_names = ("bn2", "ag2", "eps2", "rs2", "xn2_done")

            def statistics1(b):
                dve.wait_ge(s[f"ld_u{b}"], 16)
                statistics(u_sb[:, b * CH:(b + 1) * CH, :], b, norm1_names)

            def normalise1(b):
                if b >= 2:
                    dve.wait_ge(s["lnT_mm"], b - 1)
                normalise(u_sb[:, b * CH:(b + 1) * CH, :], xn[:, b % 2], b, norm1_names)

            def taps(a, bank, w, name, n, between=()):
                for k in range(TAPS - 1):
                    d = k + 1
                    if k:
                        dve.wait_ge(s[name], n + k)
                    stt(a[:, d:], ps[:, bank, 0:L - d], w[:, TAPS - 1 - d:TAPS - d], a[:, d:], ALU.mult,
                        ALU.add).then_inc(s[name], 1)
                    if k < len(between):
                        between[k]()

            def x_taps(b):
                for xt in range(2):
                    n = 2 * b + xt
                    dve.wait_ge(s["xtap"], n + 1)
                    taps(acc[:, n // GT, n % GT, :], xt, conv_sb[:, NG * GT + xt, :], "xtaps", 3 * n)

            def modulation(n):
                dve.wait_ge(s["mod_mm"], n + 1)
                mod = ps[:, 7 * n, 0:2 * KT * B].rearrange("p (k m b) -> p k m b", k=2, m=KT)
                nc.vector.tensor_copy(shift[:, n], mod[:, 0]).then_inc(s["mod_ev"], 1)
                ts(scale1[:, n], mod[:, 1], 1.0, None, ALU.add).then_inc(s["mod_ev"], 1)

            def gate_rows():
                size, sign = (xn[0:B, i, 0:2, :].rearrange("b k d -> b (k d)") for i in range(2))
                dve.wait_ge(s["gate_abs"], 1)
                ts(sign, ps[0:B, 2, :], 0.0, 2.0, ALU.is_ge, ALU.mult).then_inc(s["gate_sign"], 1)
                ts(size, size, 0.25, None, ALU.max).then_inc(s["gate_sign"], 1)
                dve.wait_ge(s["gate_sign"], 2)
                stt(size, sign, -1.0, size, ALU.add, ALU.mult).then_inc(s["gate_ev"], 1)

            statistics1(0)
            normalise1(0)
            dve.wait_ge(s["ld_wx"], 16)
            nc.vector.tensor_copy(wx_hi[:], wx_raw[:]).then_inc(s["wx_split"], 1)
            dve.wait_ge(s["wx_split"], 1)
            tt(wx_lo[:], wx_raw[:], wx_hi[:].bitcast(F32), ALU.subtract).then_inc(s["wx_split"], 1)
            statistics1(1)
            modulation(0)
            normalise1(1)
            statistics1(2)
            normalise1(2)
            statistics1(3)
            dve.wait_ge(s["ld_conv"], 16)
            x_taps(0)
            normalise1(3)
            for b in range(1, B):
                x_taps(b)

            dve.wait_ge(s["aln_done"], 1)
            stt(sp_a[:].rearrange("p b c h -> p (b c h)"), ps[:, 6, :], 0.0, a_exp[:], ALU.max,
                ALU.add).then_inc(s["sp_done"], 1)
            modulation(1)
            nc.vector.tensor_copy(cw_dve[:], conv_sb[:, 0:GT, 0:3]).then_inc(s["cwd"], 1)
            dve.wait_ge(s["ptok_mm"], 1)
            nc.vector.tensor_copy(p_tok[:].rearrange("p t h -> p (t h)"), ps[:, 7, :]).then_inc(s["p_copy"], 1)

            def mix_head(q, j, first):
                dve.wait_ge(s["score"], 4 * q + j + 1)
                dve.wait_ge(s["masked"], 4 * q + j + 1)
                if not first:
                    dve.wait_ge(s["intra"], q)
                tt(mix[:, j, :], ps[:, 2 + j % 2, :], decay[:, j, :], ALU.mult).then_inc(s["mixed"], 1)

            def conv_tile(g, b, t, between=()):
                n = (g * B + b) * GT + t
                dve.wait_ge(s["tap0"], n + 1)
                taps(acc[:, b % 2, t, :], PROJ_BANK[t], cw_dve[:, t, :], "taps", 3 * n, between)

            def copy_states(q, first):
                dve.wait_ge(s["state"], q + 1)
                for a in range(2):
                    src = ps[NS * a:NS * (a + 1), 6, 3 * P:3 * P + 96].rearrange("n (p t w) -> n p t w", p=2, t=3)
                    for p in range(2):
                        k = 2 * HD * p + HD * a
                        i = nc.vector.tensor_copy(st_sb[NS * a:NS * (a + 1), p, :, k:k + HD],
                                                  src[:, p, :, HD * a:HD * (a + 1)])
                    i.then_inc(s["st_copy"], 1)

            def y_combine(gq, q, b):
                x = x_tok[:, b * CH:(b + 1) * CH, bass.ds(gq * GC, GC)]
                x_later = x_tok[:, b * CH + 1:(b + 1) * CH, bass.ds(gq * GC, GC)]
                y = ps[:, 7, 0:2 * P].rearrange("p (c k w) -> p c k w", c=CH, k=2)

                def from_earlier():
                    dve.wait_ge(s["y_tok"], q + 1)
                    e = e_tok[:, b * CH + 1:(b + 1) * CH, bass.ds(gq * JH, JH)]
                    tt(y_off[:].rearrange("p c (j e) -> p c j e", j=JH),
                       y[:, 1:, 1].rearrange("p c (j e) -> p c j e", j=JH),
                       e.unsqueeze(3).to_broadcast([P, 3, JH, HD]), ALU.mult).then_inc(s["yoff_done"], 1)

                def inside():
                    dve.wait_ge(s["xd_done"], q + 1)
                    tt(x, y[:, :, 0], x, ALU.add).then_inc(s["y_mid"], 1)

                def total():
                    dve.wait_ge(s["yoff_done"], q + 1)
                    dve.wait_ge(s["y_mid"], q + 1)
                    tt(x_later, x_later, y_off[:], ALU.add).then_inc(s["y_done"], 1)

                return from_earlier, inside, total

            def w2_lower(n):
                dve.wait_ge(s["w2_hi_done"], n + 1)
                w = w2_lo[:, 2 * n:2 * n + 2, :].rearrange("p m d -> p (m d)")
                h = w2_hi[:, 2 * n:2 * n + 2, :].rearrange("p m d -> p (m d)")
                tt(w, ps[:, n, :], h.bitcast(F32), ALU.subtract).then_inc(s["w2_split"], 1)

            def step(g, b, attend=True, project=True, gq=None, gr=None, first=False):
                bq = (b - 1) % B
                q = gq * B + bq if attend else None
                if project and b == 0:
                    if attend:
                        dve.wait_ge(s["taps"], g * (3 * GT * B))
                    nc.vector.tensor_copy(cw_dve[:], conv_sb[:, bass.ds(g * GT, GT), 0:3]).then_inc(s["cwd"], 1)
                if project:
                    if b == 0:
                        dve.wait_ge(s["cwd"], g + 1)
                    conv_tile(g, b, 0)
                if attend:
                    mix_head(q, 0, first)
                    mix_head(q, 1, first)
                y_steps = y_combine(gr, gr * B + (b - 2) % B, (b - 2) % B) if gr is not None else ()
                if project:
                    conv_tile(g, b, 1, y_steps)
                else:
                    w2_lower(0)
                    for y_step in y_steps:
                        y_step()
                    w2_lower(1)
                if attend:
                    mix_head(q, 2, first)
                    mix_head(q, 3, first)
                    copy_states(q, first)
                if project:
                    conv_tile(g, b, 2)
                    conv_tile(g, b, 3)

            dve.wait_ge(s["cwd"], 1)
            conv_tile(0, 0, 0)
            conv_tile(0, 0, 1)
            gate_rows()
            conv_tile(0, 0, 2)
            conv_tile(0, 0, 3)
            for b in range(1, B):
                step(0, b, gq=0, gr=(None if b == 1 else 0), first=(b == 1))
            with dve.Fori(1, NG) as g:
                for b in range(B):
                    step(g, b, gq=(g - 1 if b == 0 else g), gr=(g - 1 if b < 2 else g))
            step(None, 0, gq=NG - 1, gr=NG - 1, project=False)

            def gate(b):
                for kt in range(KT):
                    dve.wait_ge(s["yT_mm"], KT * b + kt + 1)
                    dve.wait_ge(s["silu_z"], KT * b + kt + 1)
                    if not (isinstance(b, int) and b == 0):
                        dve.wait_ge(s["oproj"], 2 * b)
                    bank = 4 if isinstance(b, int) and b == 0 else 2
                    tt(gy[:, kt, :], ps[:, bank + kt, :], sz[:, kt, :], ALU.mult).then_inc(s["gated"], 1)

            def residual1(b):
                dve.wait_ge(s["ld_gates"], 16 * B)
                dve.wait_ge(s["ld_res"], (b + 1) * 16)
                ga = gates[:, bass.ds(b, 1), 0, :].to_broadcast([P, 2, D])
                bank = 4 if isinstance(b, int) and b == 0 else 2
                for h in range(2):
                    n = 2 * b + h
                    dve.wait_ge(s["oproj"], n + 1)
                    o = ps[:, bank + h, :].rearrange("p (c d) -> p c d", c=2)
                    if not (isinstance(b, int) and b == 0):
                        dve.wait_ge(s["x1_done"], n - 1)
                    tt(ga_out[:, h], o, ga, ALU.mult).then_inc(s["res_mul"], 1)
                for h in range(2):
                    n = 2 * b + h
                    dve.wait_ge(s["res_mul"], n + 1)
                    tt(x_tok[:, bass.ds(b * CH + 2 * h, 2), :], ga_out[:, h], u2[:, 2 * h:2 * h + 2, :],
                       ALU.add).then_inc(s["x1_done"], 1)

            def statistics2(b):
                dve.wait_ge(s["ld_c"], 16)
                dve.wait_ge(s["x1_done"], 2 * b + 2)
                statistics(x_tok[:, bass.ds(b * CH, CH), :], b, norm2_names)

            def normalise2(b):
                if not (isinstance(b, int) and b == 0):
                    dve.wait_ge(s["lnT2"], KT * b)
                normalise(x_tok[:, bass.ds(b * CH, CH), :], xn2[:], b, norm2_names)

            def h2_low(b):
                for kt in range(KT):
                    dve.wait_ge(s["h2hi_done"], KT * b + kt + 1)
                    tt(h2_lo[:, kt, :], h32b[:, kt, :], h2_hi[:, kt, :].bitcast(F32),
                       ALU.subtract).then_inc(s["h2lo_done"], 1)

            def hidden(b):
                for m in range(NM):
                    n = b * NM + m
                    dve.wait_ge(s["silu_done"], n + 1)
                    dve.wait_ge(s["hlo2"], n + 1)
                    tt(hid[:, m % 2, :], ps[:, 2 + m % 2, :], silu_sb[:, m % 2, :], ALU.mult).then_inc(s["hid_done"], 1)
                    if m:
                        hidden_low(n - 1, m - 1)
                hidden_low(b * NM + NM - 1, NM - 1)

            def hidden_low(n, m):
                dve.wait_ge(s["hhi2"], n + 1)
                tt(hid_lo[:, m, :], hid[:, m % 2, :], hid_hi[:, m, :].bitcast(F32), ALU.subtract).then_inc(s["hlo2"], 1)

            def residual2(b, c):
                n = b * CH + c
                dve.wait_ge(s["down_mm"], n + 1)
                x = x_tok[:, bass.ds(n, 1), :]
                t = gb_out[:, c % 2]
                dve.wait_ge(s["x2_done"], n + 1)
                tt(t, ps[:, 4 + c % 2, 0:D].unsqueeze(1), gates[:, bass.ds(b, 1), 1, :], ALU.mult).then_inc(s["out_mul"], 1)
                dve.wait_ge(s["out_mul"], SLOTS + n + 1)
                tt(x, x, t, ALU.add).then_inc(s["x2_done"], 1)

            def ffn_step(b, normed, ahead):
                hidden(b)
                if normed:
                    h2_low(b + 1)
                residual2(b, 0)
                if ahead:
                    gate(b + 2)
                residual2(b, 1)
                if ahead:
                    residual1(b + 2)
                    statistics2(b + 2)
                    normalise2(b + 2)
                residual2(b, 2)
                residual2(b, 3)

            for name in ("hlo2", "out_mul", "x2_done"):
                dve.sem_inc(s[name], SLOTS)
            gate(0)
            w2_lower(2)
            w2_lower(3)
            for y_step in y_combine(NG - 1, NG * B - 1, B - 1):
                y_step()
            residual1(0)
            statistics2(0)
            gate(1)
            normalise2(0)
            residual1(1)
            h2_low(0)
            statistics2(1)
            normalise2(1)
            with dve.Fori(0, B - 2) as b:
                ffn_step(b, True, True)
            ffn_step(B - 2, True, False)
            ffn_step(B - 1, False, False)

        @block.gpsimd
        def _(pool):
            gp = nc.gpsimd

            def await_unit(name, value):
                pool.wait_ge(s[name], value)
                pool.sem_inc(s["pool_waits"], 1)

            gp.memset(minus_half[:], -0.5).then_inc(s["half_set"], 1)
            gp.memset(rstd[:], 1.0).then_inc(s["half_set"], 1)
            pool.wait_ge(s["half_set"], 2)
            gp.tensor_tensor(rstd[:], rstd[:], minus_half[:], ALU.pow).then_inc(s["half_set"], 1)
            gp.memset(st_sb[:], 0.0).then_inc(s["st_zero"], 1)
            gp.memset(xs[:], 0.0).then_inc(s["xs_zero"], 1)
            pool.wait_ge(s["half_set"], 3)

            def split_tile(g, t):
                n = (g * GT + t) * 2
                gp.tensor_copy(wg_hi[:, t], wg_raw[:, t]).then_inc(s["w_split"], 1)
                await_unit("w_split", n + 1)
                gp.tensor_tensor(wg_lo[:, t], wg_raw[:, t], wg_hi[:, t].bitcast(F32), ALU.subtract).then_inc(s["w_split"], 1)

            def inverse_root(n, eps_name, name):
                await_unit(eps_name, n + 1)
                gp.tensor_tensor(rstd[:], vareps[:], minus_half[:], ALU.pow).then_inc(s[name], 1)

            def h_low(b):
                for kt in range(KT):
                    pool.wait_ge(s["hhi_done"], KT * b + kt + 1)
                    gp.tensor_tensor(ht_lo[:, kt, b * L:(b + 1) * L], h32[:, b % 2, kt, :],
                                     ht_hi[:, kt, b * L:(b + 1) * L].bitcast(F32), ALU.subtract).then_inc(s["hlo_done"], 1)

            inverse_root(0, "eps1", "rs")
            for b in range(B):
                if b + 1 < B:
                    inverse_root(b + 1, "eps1", "rs")
                h_low(b)
            pool.wait_ge(s["ld_wg"], 16)
            for t in range(GT):
                split_tile(0, t)
            pool.wait_ge(s["ld_wz"], 16)
            gp.tensor_copy(wz_hi[:], wz_raw[:]).then_inc(s["wz_split"], 1)
            pool.wait_ge(s["wz_split"], 1)
            gp.tensor_tensor(wz_lo[:], wz_raw[:], wz_hi[:].bitcast(F32), ALU.subtract).then_inc(s["wz_split"], 1)
            pool.wait_ge(s["ld_d"], 16)

            def scale_x(gq, q, b, first, second):
                if not first:
                    await_unit("state", q)
                for c in range(CH - 1):
                    n = CH - 1 - c
                    xc = x_tok[:, b * CH + c:b * CH + c + 1, bass.ds(gq * GC, GC)]
                    x4 = xc.rearrange("p t (j e) -> p t j e", j=JH).to_broadcast([P, n, JH, HD])
                    d4 = dec[:, V0[c]:V0[c] + n, b, bass.ds(gq * JH, JH)].unsqueeze(3).to_broadcast([P, n, JH, HD])
                    o4 = xds[:, b % 2, V0[c]:V0[c] + n, :].rearrange("p t (j e) -> p t j e", j=JH)
                    gp.tensor_tensor(o4, x4, d4, ALU.mult).then_inc(s["xds_done"], 1)
                if not (first or second):
                    await_unit("intra", q - 1)
                x = x_tok[:, b * CH:(b + 1) * CH, bass.ds(gq * GC, GC)]
                own = xs[:, b % 2].rearrange("p (j n) -> p j n", j=JH)[:, :, 0:P]
                own = own.rearrange("p j (c w) -> p c j w", c=CH)[:, :, :, 0:HD]
                gp.tensor_copy(own, x.rearrange("p c (j e) -> p c j e", j=JH)).then_inc(s["xs_done"], 1)
                await_unit("xs_done", q + 1)
                await_unit("xds_done", 3 * q + 3)
                x4 = x.rearrange("p c (j e) -> p c j e", j=JH)
                d4 = d_sb[:, bass.ds(gq * JH, JH)].unsqueeze(1).unsqueeze(3).to_broadcast([P, CH, JH, HD])
                gp.tensor_tensor(x4, x4, d4, ALU.mult).then_inc(s["xd_done"], 1)

            def mask(q, j):
                await_unit("exp_done", 4 * q + j + 1)
                v = decay[:, j, :].rearrange("p (c l) -> p c l", c=CH)
                gp.affine_select(out=v, in_=v, compare_op=ALU.is_ge, fill=0.0, base=0, pattern=[[0, CH], [1, P]],
                                 channel_multiplier=-1).then_inc(s["masked"], 1)

            def step(g, b, gq, first=False, split=False, ffn_tile=None):
                bq = (b - 1) % B
                q = gq * B + bq
                scale_x(gq, q, bq, first, isinstance(q, int) and q == 1)
                for j in range(JH):
                    mask(q, j)
                    if j == 1 and ffn_tile is not None:
                        split_ffn(ffn_tile)
                    if split and j % 2:
                        if j == 1:
                            await_unit("ld_wg", (g + 2) * 16)
                        for t in range(j - 1, j + 1):
                            await_unit("proj", (g * B + B - 1) * GT + t + 1)
                            split_tile(g + 1, t)

            pool.wait_ge(s["dec_done"], 1)
            pool.wait_ge(s["xs_zero"], 1)
            pool.wait_ge(s["xtok_ev"], 2 * B)
            w13r = stage[:].rearrange("p (m h k n) -> p m h k n", m=NM, h=2, k=KT)

            def split_ffn(m):
                if isinstance(m, int):
                    pool.wait_ge(s["ld_w13"], 16)
                    pool.wait_ge(s["xp_mm"], 2 * B)
                    pool.wait_ge(s["hlo_done"], KT * B)
                    pool.wait_ge(s["a_mm"], B)
                    pool.wait_ge(s["st_gates"], 16)
                hi, lo, raw = (w[:, bass.ds(m, 1)] for w in (w13_hi, w13_lo, w13r))
                gp.tensor_copy(hi, raw).then_inc(s["w13_hi_done"], 1)
                await_unit("w13_hi_done", m + 1)
                gp.tensor_tensor(lo, raw, hi.bitcast(F32), ALU.subtract).then_inc(s["w13_split"], 1)

            for b in range(1, B):
                step(0, b, 0, first=(b == 1), split=(b == B - 1), ffn_tile=(b - 2 if b > 1 else None))
            with pool.Fori(1, NG - 1) as g:
                for b in range(B):
                    step(g, b, (g - 1 if b == 0 else g), split=(b == B - 1), ffn_tile=(g + 1 if b == 1 else None))
            half = [stage[:, 0:NM * D], stage[:, NM * D:]]

            def butterfly(k):
                w = 1 << k
                src = half[k % 2].rearrange("p (n e w d) -> p n e (w d)", e=2, w=w, d=D)
                dst = half[1 - k % 2].rearrange("p (n e w d) -> p n e (w d)", e=2, w=w, d=D)
                if k:
                    pool.wait_ge(s["bfly"], 2 * k)
                gp.tensor_tensor(dst[:, :, 0], src[:, :, 0], src[:, :, 1], ALU.add).then_inc(s["bfly"], 1)
                gp.tensor_tensor(dst[:, :, 1], src[:, :, 0], src[:, :, 1], ALU.subtract).then_inc(s["bfly"], 1)

            for b in range(B):
                step(NG - 1, b, NG - 2 if b == 0 else NG - 1)
                if b == 0:
                    pool.wait_ge(s["ld_w2"], 16)
                if b < 3:
                    butterfly(b)
            step(None, 0, NG - 1)

            def y_values(b):
                gp.tensor_copy(yv[:], x_tok[:, bass.ds(b * CH, CH), :]).then_inc(s["yv_done"], 1)

            inverse_root(0, "eps2", "rs2")
            inverse_root(1, "eps2", "rs2")
            with pool.Fori(2, B) as b:
                await_unit("yT_mm", KT * b)
                y_values(b)
                inverse_root(b, "eps2", "rs2")


def _layout(i):
    import numpy as np

    f = {k: np.asarray(v) for k, v in i.items()}
    w_in = f["L0_attn_W_in"]
    conv_w = f["L0_attn_conv_w"][:, 0, :]
    nb = NH * NS
    k_major = lambda w: w.T.reshape(KT, P, -1).transpose(1, 0, 2)

    def tiles(w):
        return k_major(w).reshape(P, KT, -1, P).transpose(0, 2, 1, 3)

    bt = tiles(w_in[D:D + nb]).reshape(P, NG, 2, KT, P)
    ct = tiles(w_in[D + nb:D + 2 * nb]).reshape(P, NG, 2, KT, P)
    taps = np.concatenate([conv_w, f["L0_attn_conv_b"][:, None]], axis=1)
    xc = taps[:D].reshape(2, P, TAPS + 1)
    bc = taps[D:D + nb].reshape(NG, 2, P, TAPS + 1)
    cc = taps[D + nb:].reshape(NG, 2, P, TAPS + 1)
    groups = np.concatenate([bc, cc], axis=1).reshape(NG * GT, P, TAPS + 1)
    w1, w3 = (tiles(f[n]) for n in ("L0_ffn_W1", "L0_ffn_W3"))
    n = np.arange(P)
    had = np.array([[1.0]])
    while len(had) < P:
        had = np.block([[had, had], [had, -had]])
    consts = np.stack([np.eye(P), n[:, None] <= n[None, :], n[:, None] > n[None, :], np.ones((P, P)),
                       had / np.sqrt(HID)], axis=1).astype(np.float32)
    return {
        "u": f["L0_attn_u"].reshape(B * L, D),
        "w_bc": np.concatenate([bt, ct], axis=2).transpose(1, 0, 2, 3, 4),
        "w_x": tiles(w_in[:D]),
        "w_a": k_major(w_in[2 * D + 2 * nb:]),
        "w_z": tiles(w_in[D + 2 * nb:2 * D + 2 * nb]),
        "conv": np.concatenate([groups, xc], axis=0).transpose(1, 0, 2),
        "d_rows": np.broadcast_to(f["L0_attn_D"], (P, NH)),
        "z_bias": f["L0_attn_z_bias"].reshape(2, P).T,
        "w_out": k_major(f["L0_attn_W_out"]),
        "w13": np.stack([w1, w3], axis=2).reshape(P, -1),
        "w2": f["L0_ffn_W2"].T.reshape(NM, P, D).transpose(1, 0, 2).reshape(P, -1),
        "c_t": f["L0_c"].T.reshape(KT, P, B).transpose(1, 0, 2),
        "wmod": f["L0_wmod"].reshape(KT, P, 6 * D).transpose(1, 0, 2),
        "consts": consts,
    }


def kernel(**inputs):
    import numpy as _np
    import concourse.bacc as _bacc
    from concourse import mybir as _mybir
    from concourse.bass_utils import run_bass_kernel_spmd as _run

    nc = _bacc.Bacc("TRN2", target_bir_lowering=False, num_devices=1)
    arrays, args = {}, []
    for name, a in _layout(inputs).items():
        a = _np.ascontiguousarray(a)
        arrays[f"in_{name}"] = a
        args.append(nc.dram_tensor(f"in_{name}", a.shape, _mybir.dt.from_np(a.dtype), kind="ExternalInput").ap())
    args.append(nc.dram_tensor("out_0", (B * L, D), _mybir.dt.float32, kind="ExternalOutput").ap())
    args.append(nc.dram_tensor("running_sums", (B * NH, L), _mybir.dt.float32).ap())
    args.append(nc.dram_tensor("gate_rows", (B, 2 * D), _mybir.dt.float32).ap())
    adaln_ssm_ffn_kernel(nc, *args)
    r = _run(nc, [arrays], core_ids=[0])
    return r.results[0]["out_0"].reshape(B, L, D)
```
